# Optimizing a Trainium2 kernel written in Bass

```python
import numpy as np
import jax
import jax.numpy as jnp

def _softmax(x, axis=-1):
    return jax.nn.softmax(x, axis=axis)

def _gelu(x):
    return jax.nn.gelu(x, approximate=True)

def _silu(x):
    return jax.nn.silu(x)

def _sigmoid(x):
    return jax.nn.sigmoid(x)

def _layernorm(x, axis=-1, eps=1e-05):
    m = jnp.mean(x, axis=axis, keepdims=True)
    v = jnp.var(x, axis=axis, keepdims=True)
    return (x - m) / jnp.sqrt(v + eps)

def _scatter_add(tgt, idx, src, axis=0):
    return tgt.at[idx].add(src)

def _segment_sum(src, seg, n):
    return jax.ops.segment_sum(src, seg, n)
kernel_name = 'mk_perceiver_d2_seqx_r2_f451db'

def setup_inputs(seed: int=0):
    np.random.seed(seed)
    _w = jnp.asarray

    def _rec_inputs():
        import jax
        import jax.numpy as jnp
        _rk = jax.random.key(seed)
        x = -0.0005146 + 1 * jax.random.normal(jax.random.fold_in(_rk, 1), (32, 32, 512), jnp.float32)
        _lenS = 32 - jax.random.randint(jax.random.fold_in(_rk, 7), (32,), 0, max(1, 32 // 4) + 1, jnp.int32)
        _lenS2 = 257 - jax.random.randint(jax.random.fold_in(_rk, 8), (32,), 0, max(1, 257 // 4) + 1, jnp.int32)
        _ctx_768P = jax.random.normal(jax.random.fold_in(_rk, 11), (32, 16, 384), jnp.float32)
        _ctx_768c = jax.random.dirichlet(jax.random.fold_in(_rk, 511), 0.3 * jnp.ones((16,), jnp.float32), (32, 257))
        _ctx_768t = jnp.einsum('bsk,bkd->bsd', _ctx_768c, _ctx_768P)
        _ctx_768t = _ctx_768t * jax.lax.rsqrt(jnp.mean(jnp.square(_ctx_768t)) + 1e-12) * 0.953939
        ctx_768 = -0.00040386 + 0.999972 * (_ctx_768t + 0.3 * jax.random.normal(jax.random.fold_in(_rk, 611), (32, 257, 384), jnp.float32))
        _validS = jnp.arange(32)[None, :] < _lenS[:, None]
        _validS2 = jnp.arange(257)[None, :] < _lenS2[:, None]
        _causal = jnp.tril(jnp.ones((32, 32), dtype=bool))
        mask_BxS2_bk0 = jnp.logical_not(jnp.broadcast_to(_validS2[:, :], (32, 257)))
        return (x, ctx_768, mask_BxS2_bk0)
    x, ctx_768, mask_BxS2_bk0 = _rec_inputs()

    def _L0_xattn_setup():
        import jax, jax.numpy as jnp
        import numpy as np
        DIM_IN, DIM_LAT, DIM_HEAD = (384, 512, 64)
        INNER = max(DIM_LAT, DIM_IN)
        HEADS = INNER // DIM_HEAD
        SCALE = DIM_HEAD ** (-0.5)
        RMS_EPS = 1e-08
        LN_EPS = 1e-05

        def layernorm(x, g, b):
            mu = jnp.mean(x, axis=-1, keepdims=True)
            var = jnp.mean((x - mu) ** 2, axis=-1, keepdims=True)
            return (x - mu) * jax.lax.rsqrt(var + LN_EPS) * g + b

        def rmsnorm(x, gamma):
            norm = jnp.sqrt(jnp.sum(x * x, axis=-1, keepdims=True)) * x.shape[-1] ** (-0.5)
            return x / jnp.maximum(norm, RMS_EPS) * gamma
        key = jax.random.key(seed)
        ks = jax.random.split(key, 12)
        b, n, m = (4, 2048, 256)
        x = jax.random.normal(ks[0], (b, n, DIM_IN), jnp.float32)
        latents = jax.random.normal(ks[1], (b, m, DIM_LAT), jnp.float32)
        mask = jax.random.randint(ks[2], (b, n), 0, 2).astype(bool)
        s = lambda k, sh, fan: jax.random.normal(k, sh, jnp.float32) * fan ** (-0.5)
        return {'x': x, 'latents': latents, 'mask': mask, 'ln_x_g': jnp.ones((DIM_IN,), jnp.float32), 'ln_x_b': jnp.zeros((DIM_IN,), jnp.float32), 'ln_l_g': jnp.ones((DIM_LAT,), jnp.float32), 'ln_l_b': jnp.zeros((DIM_LAT,), jnp.float32), 'qn_g': jnp.ones((DIM_HEAD,), jnp.float32), 'kn_g': jnp.ones((DIM_HEAD,), jnp.float32), 'Wq': s(ks[3], (INNER, DIM_LAT), DIM_LAT), 'Wkv': s(ks[4], (2 * INNER, DIM_IN), DIM_IN), 'Wlkv': s(ks[5], (2 * INNER, DIM_LAT), DIM_LAT), 'Wo': s(ks[6], (DIM_LAT, INNER), INNER), 'bo': jnp.zeros((DIM_LAT,), jnp.float32)}
    _L0_xattn_all = _L0_xattn_setup()
    _L0_xattn_in = {k: v for k, v in _L0_xattn_all.items() if k in ('ln_x_g', 'ln_x_b', 'ln_l_g', 'ln_l_b', 'qn_g', 'kn_g', 'Wq', 'Wkv', 'Wlkv', 'Wo', 'bo')}
    del _L0_xattn_all

    def _L0_attn_setup():
        import jax, jax.numpy as jnp
        import numpy as np
        B, S, D = (8, 1024, 512)
        key = jax.random.key(seed)
        kx, kw, kb = jax.random.split(key, 3)
        x = jax.random.normal(kx, (B, S, D), dtype=jnp.float32)
        W = jax.random.normal(kw, (3 * D, D), dtype=jnp.float32) * (1.0 / np.sqrt(D))
        b = jax.random.normal(kb, (3 * D,), dtype=jnp.float32) * 0.01
        return {'x': x, 'W': W, 'b': b}
    _L0_attn_all = _L0_attn_setup()
    _L0_attn_in = {k: v for k, v in _L0_attn_all.items() if k in ('W', 'b')}
    del _L0_attn_all

    def _L0_ffn_setup():
        import jax, jax.numpy as jnp
        import numpy as np
        B, L, H = (32, 256, 512)
        E, R, TOP_K = (8, 16, 2)

        def _gates(cls, router_w):
            logits = jnp.einsum('bh,eh->be', cls, router_w)
            top_vals, top_idx = jax.lax.top_k(logits, TOP_K)
            mask = jnp.full_like(logits, -jnp.inf)
            rows = jnp.arange(logits.shape[0])[:, None]
            mask = mask.at[rows, top_idx].set(top_vals)
            return jax.nn.softmax(mask, axis=1)
        key = jax.random.key(seed)
        k1, k2, k3, k4 = jax.random.split(key, 4)
        x = jax.random.normal(k1, (B, L, H), dtype=jnp.float32)
        router_w = jax.random.normal(k2, (E, H), dtype=jnp.float32) * 0.02
        lora_down = jax.random.normal(k3, (E, R, H), dtype=jnp.float32) * (1.0 / np.sqrt(H))
        lora_up = jax.random.normal(k4, (E, H, R), dtype=jnp.float32) * (1.0 / np.sqrt(R))
        return {'x': x, 'router_w': router_w, 'lora_down': lora_down, 'lora_up': lora_up}
    _L0_ffn_all = _L0_ffn_setup()
    _L0_ffn_in = {k: v for k, v in _L0_ffn_all.items() if k in ('router_w', 'lora_down', 'lora_up')}
    del _L0_ffn_all

    def _L1_xattn_setup():
        import math
        import jax, jax.numpy as jnp
        import numpy as np
        B, SQ, SKV = (4, 1024, 1024)
        D_EMBED, D_CROSS, D_ATT, N_HEADS = (512, 384, 512, 16)
        D_HEAD = D_ATT // N_HEADS

        def _split_heads(t):
            b, s, _ = t.shape
            return t.reshape(b, s, N_HEADS, D_HEAD).transpose(0, 2, 1, 3)
        key = jax.random.key(seed)
        ks = jax.random.split(key, 10)
        s_e = 1.0 / math.sqrt(D_EMBED)
        s_c = 1.0 / math.sqrt(D_CROSS)
        s_a = 1.0 / math.sqrt(D_ATT)
        return {'x': jax.random.normal(ks[0], (B, SQ, D_EMBED), jnp.float32), 'y': jax.random.normal(ks[1], (B, SKV, D_CROSS), jnp.float32), 'Wq': jax.random.normal(ks[2], (D_EMBED, D_ATT), jnp.float32) * s_e, 'bq': jax.random.normal(ks[3], (D_ATT,), jnp.float32) * 0.01, 'Wk': jax.random.normal(ks[4], (D_CROSS, D_ATT), jnp.float32) * s_c, 'bk': jax.random.normal(ks[5], (D_ATT,), jnp.float32) * 0.01, 'Wv': jax.random.normal(ks[6], (D_CROSS, D_ATT), jnp.float32) * s_c, 'bv': jax.random.normal(ks[7], (D_ATT,), jnp.float32) * 0.01, 'Wo': jax.random.normal(ks[8], (D_ATT, D_EMBED), jnp.float32) * s_a, 'bo': jax.random.normal(ks[9], (D_EMBED,), jnp.float32) * 0.01}
    _L1_xattn_all = _L1_xattn_setup()
    _L1_xattn_in = {k: v for k, v in _L1_xattn_all.items() if k in ('Wq', 'bq', 'Wk', 'bk', 'Wv', 'bv', 'Wo', 'bo')}
    del _L1_xattn_all

    def _L1_attn_setup():
        import jax, jax.numpy as jnp
        import numpy as np
        N_HEAD = 16
        N_EMBD = 512
        HEAD_DIM = N_EMBD // N_HEAD
        ROPE_BASE = 10000.0

        def _rotary_cos_sin(T, dim, dtype=jnp.float32):
            inv_freq = 1.0 / ROPE_BASE ** (jnp.arange(0, dim, 2, dtype=jnp.float32) / dim)
            freqs = jnp.arange(T, dtype=jnp.float32)[:, None] * inv_freq[None, :]
            cos = jnp.cos(freqs).astype(jnp.bfloat16).astype(dtype)
            sin = jnp.sin(freqs).astype(jnp.bfloat16).astype(dtype)
            return (cos[None, :, None, :], sin[None, :, None, :])

        def _apply_rotary(x, cos, sin):
            d = x.shape[3] // 2
            x1, x2 = (x[..., :d], x[..., d:])
            y1 = x1 * cos + x2 * sin
            y2 = -x1 * sin + x2 * cos
            return jnp.concatenate([y1, y2], axis=3).astype(x.dtype)
        key = jax.random.key(seed)
        ks = jax.random.split(key, 8)
        B, T, C = (2, 1024, N_EMBD)
        scale = C ** (-0.5)
        x = jax.random.normal(ks[0], (B, T, C), dtype=jnp.float32)
        Wq1 = jax.random.normal(ks[1], (C, C), dtype=jnp.float32) * scale
        Wk1 = jax.random.normal(ks[2], (C, C), dtype=jnp.float32) * scale
        Wq2 = jax.random.normal(ks[3], (C, C), dtype=jnp.float32) * scale
        Wk2 = jax.random.normal(ks[4], (C, C), dtype=jnp.float32) * scale
        Wv = jax.random.normal(ks[5], (C, C), dtype=jnp.float32) * scale
        Wout = jax.random.normal(ks[6], (C, C), dtype=jnp.float32) * scale
        return {'x': x, 'Wq1': Wq1, 'Wk1': Wk1, 'Wq2': Wq2, 'Wk2': Wk2, 'Wv': Wv, 'Wout': Wout}
    _L1_attn_all = _L1_attn_setup()
    _L1_attn_in = {k: v for k, v in _L1_attn_all.items() if k in ('Wq1', 'Wk1', 'Wq2', 'Wk2', 'Wv', 'Wout')}
    del _L1_attn_all

    def _L1_ffn_setup():
        import jax, jax.numpy as jnp
        import numpy as np
        HIDDEN = 512
        INTER = 1024
        N_EXPERTS = 8
        TOP_K = 2
        NORM_TOPK = True
        key = jax.random.key(seed)
        ks = jax.random.split(key, 5)
        B, S = (2, 2048)
        hidden_states = jax.random.normal(ks[0], (B, S, HIDDEN), dtype=jnp.float32)
        router_w = jax.random.normal(ks[1], (N_EXPERTS, HIDDEN), dtype=jnp.float32) * HIDDEN ** (-0.5)
        wg = jax.random.normal(ks[2], (N_EXPERTS, INTER, HIDDEN), dtype=jnp.float32) * HIDDEN ** (-0.5)
        wu = jax.random.normal(ks[3], (N_EXPERTS, INTER, HIDDEN), dtype=jnp.float32) * HIDDEN ** (-0.5)
        wd = jax.random.normal(ks[4], (N_EXPERTS, HIDDEN, INTER), dtype=jnp.float32) * INTER ** (-0.5)
        return {'hidden_states': hidden_states, 'router_w': router_w, 'wg': wg, 'wu': wu, 'wd': wd}
    _L1_ffn_all = _L1_ffn_setup()
    _L1_ffn_in = {k: v for k, v in _L1_ffn_all.items() if k in ('router_w', 'wg', 'wu', 'wd')}
    del _L1_ffn_all
    return {'x': x, 'ctx_768': ctx_768, 'mask_BxS2_bk0': mask_BxS2_bk0, 'L0_xattn_ln_x_g': _L0_xattn_in['ln_x_g'], 'L0_xattn_ln_x_b': _L0_xattn_in['ln_x_b'], 'L0_xattn_ln_l_g': _L0_xattn_in['ln_l_g'], 'L0_xattn_ln_l_b': _L0_xattn_in['ln_l_b'], 'L0_xattn_qn_g': _L0_xattn_in['qn_g'], 'L0_xattn_kn_g': _L0_xattn_in['kn_g'], 'L0_xattn_Wq': _L0_xattn_in['Wq'], 'L0_xattn_Wkv': _L0_xattn_in['Wkv'], 'L0_xattn_Wlkv': _L0_xattn_in['Wlkv'], 'L0_xattn_Wo': _L0_xattn_in['Wo'], 'L0_xattn_bo': _L0_xattn_in['bo'], 'L0_attn_W': _L0_attn_in['W'], 'L0_attn_b': _L0_attn_in['b'], 'L0_ffn_router_w': _L0_ffn_in['router_w'], 'L0_ffn_lora_down': _L0_ffn_in['lora_down'], 'L0_ffn_lora_up': _L0_ffn_in['lora_up'], 'L1_xattn_Wq': _L1_xattn_in['Wq'], 'L1_xattn_bq': _L1_xattn_in['bq'], 'L1_xattn_Wk': _L1_xattn_in['Wk'], 'L1_xattn_bk': _L1_xattn_in['bk'], 'L1_xattn_Wv': _L1_xattn_in['Wv'], 'L1_xattn_bv': _L1_xattn_in['bv'], 'L1_xattn_Wo': _L1_xattn_in['Wo'], 'L1_xattn_bo': _L1_xattn_in['bo'], 'L1_attn_Wq1': _L1_attn_in['Wq1'], 'L1_attn_Wk1': _L1_attn_in['Wk1'], 'L1_attn_Wq2': _L1_attn_in['Wq2'], 'L1_attn_Wk2': _L1_attn_in['Wk2'], 'L1_attn_Wv': _L1_attn_in['Wv'], 'L1_attn_Wout': _L1_attn_in['Wout'], 'L1_ffn_router_w': _L1_ffn_in['router_w'], 'L1_ffn_wg': _L1_ffn_in['wg'], 'L1_ffn_wu': _L1_ffn_in['wu'], 'L1_ffn_wd': _L1_ffn_in['wd']}

def reference(x, ctx_768, mask_BxS2_bk0, L0_xattn_ln_x_g, L0_xattn_ln_x_b, L0_xattn_ln_l_g, L0_xattn_ln_l_b, L0_xattn_qn_g, L0_xattn_kn_g, L0_xattn_Wq, L0_xattn_Wkv, L0_xattn_Wlkv, L0_xattn_Wo, L0_xattn_bo, L0_attn_W, L0_attn_b, L0_ffn_router_w, L0_ffn_lora_down, L0_ffn_lora_up, L1_xattn_Wq, L1_xattn_bq, L1_xattn_Wk, L1_xattn_bk, L1_xattn_Wv, L1_xattn_bv, L1_xattn_Wo, L1_xattn_bo, L1_attn_Wq1, L1_attn_Wk1, L1_attn_Wq2, L1_attn_Wk2, L1_attn_Wv, L1_attn_Wout, L1_ffn_router_w, L1_ffn_wg, L1_ffn_wu, L1_ffn_wd):
    import jax
    import jax.numpy as jnp

    def _L0_xattn_ref(x, latents, mask, ln_x_g, ln_x_b, ln_l_g, ln_l_b, qn_g, kn_g, Wq, Wkv, Wlkv, Wo, bo):
        import jax, jax.numpy as jnp
        import numpy as np
        DIM_IN, DIM_LAT, DIM_HEAD = (384, 512, 64)
        INNER = max(DIM_LAT, DIM_IN)
        HEADS = INNER // DIM_HEAD
        SCALE = DIM_HEAD ** (-0.5)
        RMS_EPS = 1e-08
        LN_EPS = 1e-05

        def layernorm(x, g, b):
            mu = jnp.mean(x, axis=-1, keepdims=True)
            var = jnp.mean((x - mu) ** 2, axis=-1, keepdims=True)
            return (x - mu) * jax.lax.rsqrt(var + LN_EPS) * g + b

        def rmsnorm(x, gamma):
            norm = jnp.sqrt(jnp.sum(x * x, axis=-1, keepdims=True)) * x.shape[-1] ** (-0.5)
            return x / jnp.maximum(norm, RMS_EPS) * gamma
        b, n, _ = x.shape
        m = latents.shape[1]
        xn = layernorm(x, ln_x_g, ln_x_b)
        ln = layernorm(latents, ln_l_g, ln_l_b)
        q = ln @ Wq.T
        kv = jnp.concatenate([xn @ Wkv.T, ln @ Wlkv.T], axis=1)
        k, v = (kv[..., :INNER], kv[..., INNER:])
        split_heads = lambda t: t.reshape(t.shape[0], t.shape[1], HEADS, DIM_HEAD).transpose(0, 2, 1, 3)
        q, k, v = (split_heads(q), split_heads(k), split_heads(v))
        qn = rmsnorm(q, qn_g) * SCALE
        kn = rmsnorm(k, kn_g)
        attn = jnp.einsum('bhid,bhjd->bhij', qn, kn)
        full_mask = jnp.pad(mask, ((0, 0), (0, m)), constant_values=True)
        attn = jnp.where(full_mask[:, None, None, :], attn, -jnp.finfo(attn.dtype).max)
        attn = jax.nn.softmax(attn, axis=-1)
        out = jnp.einsum('bhij,bhjd->bhid', attn, v)
        out = out.transpose(0, 2, 1, 3).reshape(b, m, INNER)
        return out @ Wo.T + bo

    def _L0_attn_ref(x, W, b):
        import jax, jax.numpy as jnp
        import numpy as np
        B, S, D = (8, 1024, 512)
        qkv = jnp.einsum('bsd,fd->bsf', x, W) + b
        q, k, v = jnp.split(qkv, 3, axis=-1)
        attn = jnp.einsum('bik,bjk->bij', q, k) / k.shape[-1]
        attn = jax.nn.softmax(attn, axis=1)
        out = jnp.einsum('bij,bjk->bik', attn, v)
        return out

    def _L0_ffn_ref(x, router_w, lora_down, lora_up):
        import jax, jax.numpy as jnp
        import numpy as np
        B, L, H = (32, 256, 512)
        E, R, TOP_K = (8, 16, 2)

        def _gates(cls, router_w):
            logits = jnp.einsum('bh,eh->be', cls, router_w)
            top_vals, top_idx = jax.lax.top_k(logits, TOP_K)
            mask = jnp.full_like(logits, -jnp.inf)
            rows = jnp.arange(logits.shape[0])[:, None]
            mask = mask.at[rows, top_idx].set(top_vals)
            return jax.nn.softmax(mask, axis=1)
        gates = _gates(x[:, 0, :], router_w)
        down = jnp.einsum('blh,erh->bler', x, lora_down)
        weighted = jnp.einsum('bler,ehr,be->blh', down, lora_up, gates)
        return x + weighted

    def _L1_xattn_ref(x, y, Wq, bq, Wk, bk, Wv, bv, Wo, bo):
        import math
        import jax, jax.numpy as jnp
        import numpy as np
        B, SQ, SKV = (4, 1024, 1024)
        D_EMBED, D_CROSS, D_ATT, N_HEADS = (512, 384, 512, 16)
        D_HEAD = D_ATT // N_HEADS

        def _split_heads(t):
            b, s, _ = t.shape
            return t.reshape(b, s, N_HEADS, D_HEAD).transpose(0, 2, 1, 3)
        q = _split_heads(x @ Wq + bq)
        k = _split_heads(y @ Wk + bk)
        v = _split_heads(y @ Wv + bv)
        scale = 1.0 / math.sqrt(D_HEAD)
        scores = jnp.einsum('bhqd,bhkd->bhqk', q, k) * scale
        weights = jax.nn.softmax(scores, axis=-1)
        out = jnp.einsum('bhqk,bhkd->bhqd', weights, v)
        out = out.transpose(0, 2, 1, 3).reshape(x.shape[0], x.shape[1], D_ATT)
        return out @ Wo + bo

    def _L1_attn_ref(x, Wq1, Wk1, Wq2, Wk2, Wv, Wout):
        import jax, jax.numpy as jnp
        import numpy as np
        N_HEAD = 16
        N_EMBD = 512
        HEAD_DIM = N_EMBD // N_HEAD
        ROPE_BASE = 10000.0

        def _rotary_cos_sin(T, dim, dtype=jnp.float32):
            inv_freq = 1.0 / ROPE_BASE ** (jnp.arange(0, dim, 2, dtype=jnp.float32) / dim)
            freqs = jnp.arange(T, dtype=jnp.float32)[:, None] * inv_freq[None, :]
            cos = jnp.cos(freqs).astype(jnp.bfloat16).astype(dtype)
            sin = jnp.sin(freqs).astype(jnp.bfloat16).astype(dtype)
            return (cos[None, :, None, :], sin[None, :, None, :])

        def _apply_rotary(x, cos, sin):
            d = x.shape[3] // 2
            x1, x2 = (x[..., :d], x[..., d:])
            y1 = x1 * cos + x2 * sin
            y2 = -x1 * sin + x2 * cos
            return jnp.concatenate([y1, y2], axis=3).astype(x.dtype)
        B, T, C = x.shape
        H, D = (N_HEAD, HEAD_DIM)

        def proj(W):
            return (x @ W.T).reshape(B, T, H, D)
        q1, k1 = (proj(Wq1), proj(Wk1))
        q2, k2 = (proj(Wq2), proj(Wk2))
        v = proj(Wv)
        cos, sin = _rotary_cos_sin(T, D, x.dtype)
        q1, k1 = (_apply_rotary(q1, cos, sin), _apply_rotary(k1, cos, sin))
        q2, k2 = (_apply_rotary(q2, cos, sin), _apply_rotary(k2, cos, sin))
        s1 = jnp.einsum('bqhd,bkhd->bhqk', q1, k1)
        s2 = jnp.einsum('bqhd,bkhd->bhqk', q2, k2)
        causal = jnp.tril(jnp.ones((T, T), dtype=bool))
        pattern = jnp.where(causal[None, None], s1 / D * (s2 / D), 0.0)
        y = jnp.einsum('bhqk,bkhd->bqhd', pattern, v).reshape(B, T, C)
        return y @ Wout.T

    def _L1_ffn_ref(hidden_states, router_w, wg, wu, wd):
        import jax, jax.numpy as jnp
        import numpy as np
        HIDDEN = 512
        INTER = 1024
        N_EXPERTS = 8
        TOP_K = 2
        NORM_TOPK = True
        B, S, H = hidden_states.shape
        T = B * S
        x = hidden_states.reshape(T, H)
        logits = jnp.einsum('th,eh->te', x, router_w)
        probs = jax.nn.softmax(logits.astype(jnp.float32), axis=-1)
        top_w, top_idx = jax.lax.top_k(probs, TOP_K)
        if NORM_TOPK:
            top_w = top_w / jnp.sum(top_w, axis=-1, keepdims=True)
        top_w = top_w.astype(x.dtype)
        combine = jnp.zeros((T, N_EXPERTS), dtype=x.dtype)
        combine = combine.at[jnp.arange(T)[:, None], top_idx].add(top_w)
        g = jnp.einsum('th,eih->eti', x, wg)
        u = jnp.einsum('th,eih->eti', x, wu)
        mid = jax.nn.silu(g) * u
        expert_out = jnp.einsum('eti,ehi->eth', mid, wd)
        out = jnp.einsum('eth,te->th', expert_out, combine)
        return out.reshape(B, S, H)
    x = x + _L0_xattn_ref(ctx_768, _layernorm(x, axis=-1), mask_BxS2_bk0, L0_xattn_ln_x_g, L0_xattn_ln_x_b, L0_xattn_ln_l_g, L0_xattn_ln_l_b, L0_xattn_qn_g, L0_xattn_kn_g, L0_xattn_Wq, L0_xattn_Wkv, L0_xattn_Wlkv, L0_xattn_Wo, L0_xattn_bo)
    x = x + _L0_attn_ref(_layernorm(x, axis=-1), L0_attn_W, L0_attn_b)
    x = x + _L0_ffn_ref(_layernorm(x, axis=-1), L0_ffn_router_w, L0_ffn_lora_down, L0_ffn_lora_up)
    x = x + _L1_xattn_ref(_layernorm(x, axis=-1), ctx_768, L1_xattn_Wq, L1_xattn_bq, L1_xattn_Wk, L1_xattn_bk, L1_xattn_Wv, L1_xattn_bv, L1_xattn_Wo, L1_xattn_bo)
    x = x + _L1_attn_ref(_layernorm(x, axis=-1), L1_attn_Wq1, L1_attn_Wk1, L1_attn_Wq2, L1_attn_Wk2, L1_attn_Wv, L1_attn_Wout)
    x = x + _L1_ffn_ref(_layernorm(x, axis=-1), L1_ffn_router_w, L1_ffn_wg, L1_ffn_wu, L1_ffn_wd)
    return x

_drawn_inputs = setup_inputs


def setup_inputs(seed=0):
    import zlib

    import numpy as np

    out = dict(_drawn_inputs(seed))
    spreads = {'L0_xattn_ln_x_g': (1.0, 0.2),
     'L0_xattn_ln_x_b': (0.0, 0.1),
     'L0_xattn_ln_l_g': (1.0, 0.2),
     'L0_xattn_ln_l_b': (0.0, 0.1),
     'L0_xattn_qn_g': (1.0, 0.2),
     'L0_xattn_kn_g': (1.0, 0.2),
     'L0_xattn_bo': (0.0, 0.1)}
    factors = {'L1_xattn_bq': 26.7, 'L1_xattn_bk': 64.0, 'L1_xattn_bv': 6.376, 'L1_xattn_bo': 6.727}
    for name, (base, spread) in spreads.items():
        noise = np.random.default_rng([zlib.crc32(name.encode()), seed]).standard_normal(out[name].shape)
        drawn = base * np.exp(spread * noise) if base else spread * noise
        out[name] = jnp.asarray(drawn.astype(out[name].dtype))
    for name, factor in factors.items():
        out[name] = (out[name] * factor).astype(out[name].dtype)
    return out
```

```python
from contextlib import ExitStack

import numpy as np

import concourse.bass as bass
from concourse import mybir

F32, F16, BF16 = mybir.dt.float32, mybir.dt.float16, mybir.dt.bfloat16
U8, I32 = mybir.dt.uint8, mybir.dt.int32
ALU = mybir.AluOpType
ACT = mybir.ActivationFunctionType
AX = mybir.AxisListType
ds = bass.ds

P = 128
B, S, D = 32, 32, 512
SC, DC = 257, 384
CK, XK = D // P, DC // P
TOK = B * S
NT = TOK // P
BPT = P // S
FULL = SC - 1
KEYS = FULL + S + 1
H0, HD0 = 8, 64
H1, HD1 = 16, 32
E0, R0 = 8, 16
E1, INTER = 8, 1024
IK = INTER // P
EPS = 1e-5
WS = 16.0
MASKED = -1e30

WCOLS = [("q0", CK * D), ("lkv0", CK * 2 * D), ("kv0", XK * 2 * D), ("k1", XK * D), ("v1", XK * D),
         ("o0", CK * D), ("qkv0", CK * 3 * D), ("down", CK * E0 * R0), ("up", D), ("r0", CK * E0), ("q1", CK * D),
         ("o1", CK * D), ("pq1", CK * D), ("pk1", CK * D), ("pq2", CK * D), ("pk2", CK * D), ("pv", CK * D),
         ("out1", CK * D), ("r1", CK * E1)]
WAT = {}
_at = 0
for _n, _c in WCOLS:
    WAT[_n] = _at
    _at += _c
WTOTAL = _at
EXPERT = 2 * CK * INTER + IK * D
STAGE = 2048

VCOLS = [("lng", CK), ("lnb", CK), ("lxg", XK), ("lxb", XK), ("qg", 1), ("kg", 1), ("bqk0", 2 * CK),
         ("bq1", CK), ("bk1", CK), ("bv1", CK)]
VAT = {}
_at = 0
for _n, _c in VCOLS:
    VAT[_n] = _at
    _at += _c
VTOTAL = _at


STARTS = {"kh0": 1, "kh1": 1, "vl_lo": 1, "hT0_lo": 1, "hT1_lo": 1, "vlat_out0": 16, "vlat_out1": 16,
          "c0_kh": 1, "c0_vlo": 1, "c0_ktlo": 1, "c0_ss": 1, "c0_olo": 2, "c0_exp": 2, "c0_kt": 1, "c0_pt": 1,
          "c0_z": 3, "c0_zlo": 1, "d_klo": 1, "d_vlo": 1, "d_z": 1, "d_exp": 1, "d_pt": 1,
          "e_mf": 2, "e_x": 1, "e_ylo": 1, "e_given": 1, "e_turned": 1, "e_down": 1}


class Signals:

    def __init__(self, nc, starts, stage):
        self.nc, self.made, self.starts, self.stage = nc, {}, starts, stage

    def begin(self, engine, *names):
        for name in names:
            engine.sem_inc(self[name], self.starts[name])

    def passed(self, engine, who):
        engine.sem_inc(self[f"{self.stage}_{who}_passed"], 1)

    def __getitem__(self, name):
        if name not in self.made:
            self.made[name] = self.nc.alloc_semaphore(name)
        return self.made[name]


def product(pe, out, left, right, first=True, last=True):
    lh, ll = left
    rh, rl = right
    pe.matmul(out, lh, rh, start=first, stop=False)
    pe.matmul(out, lh, rl, start=False, stop=False)
    return pe.matmul(out, ll, rh, start=False, stop=last)


class Norm:

    def __init__(self, sig, name, work):
        self.sig = sig
        self.stat, self.rstd, self.done = sig[name + "_stat"], sig[name + "_rstd"], sig[name + "_norm"]
        self.w = work

    def stats(self, dve, u, n, src, rows=P):
        st, mv, _ = self.w[u]
        dve.bn_stats(st[0:rows, :], src).then_inc(self.stat, 1)
        dve.wait_ge(self.stat, n * 3 + 1)
        self.sig.passed(dve, "dve")
        dve.bn_aggr(mv[0:rows, 0:2], st[0:rows, :]).then_inc(self.stat, 1)
        dve.wait_ge(self.stat, n * 3 + 2)
        dve.tensor_scalar(mv[0:rows, 2:3], mv[0:rows, 1:2], EPS, None, ALU.add).then_inc(self.stat, 1)

    def power(self, pool, u, n, half, rows=P):
        _, mv, rs = self.w[u]
        pool.wait_ge(self.stat, n * 3 + 3)
        pool.tensor_tensor(rs[0:rows, :], mv[0:rows, 2:3], half[0:rows, 0:1], ALU.pow).then_inc(self.rstd, 1)

    def scale(self, dve, u, n, src, y, rows=P):
        _, mv, rs = self.w[u]
        dve.wait_ge(self.rstd, n + 1)
        dve.tensor_scalar(y, src, mv[0:rows, 0:1], rs[0:rows, 0:1], ALU.subtract, ALU.mult).then_inc(self.done, 1)


def stage(st, program):
    nc = st["nc"]
    st["sig"] = Signals(nc, STARTS, program.__name__)
    program(st)
    nc.clear_and_free_semaphores(list(st["sig"].made.values()))
    nc.all_engine_barrier()


def perceiver(nc, d, out):
    ctx = ExitStack()
    with ctx:
        sb = lambda c, name, shape, dt=F32: c.enter_context(nc.sbuf_tensor(name, shape, dt))
        X = sb(ctx, "X", [P, NT, D])
        XT = sb(ctx, "XT", [P, 2, CK, TOK], F16)
        vecs = sb(ctx, "vecs", [P, VTOTAL])
        vecs16 = sb(ctx, "vecs16", [P, VTOTAL])
        ident = sb(ctx, "ident", [P, P])
        LG = sb(ctx, "LG", [P, NT, E1])
        mhalf = sb(ctx, "mhalf", [P, 8])
        work = [[sb(ctx, f"st{u}", [P, 6]), sb(ctx, f"mv{u}", [P, 4]), sb(ctx, f"rs{u}", [P, 1])] for u in range(2)]
        st = dict(nc=nc, d=d, out=out, sb=sb, X=X, XT=XT, LG=LG, vecs=vecs, vecs16=vecs16, ident=ident,
                  mhalf=mhalf, work=work, ctx=ctx)
        st["vlat"] = nc.dram_tensor("vlat", (TOK, 2 * D), F16, kind="Internal").ap()
        st["vrem"] = nc.dram_tensor("vrem", (B, 2 * D), F16, kind="Internal").ap()
        st["vrem1"] = nc.dram_tensor("vrem1", (B, 2 * D), F16, kind="Internal").ap()
        st["K1R"] = sb(ctx, "K1R", [P, 2, CK, B], F16)
        with ExitStack() as c12:
            st["KL"] = sb(c12, "KL", [P, 2, CK, TOK], F16)
            st["KR"] = sb(c12, "KR", [P, 2, CK, B], F16)
            st["W12"] = sb(c12, "W12", [P, 2, XK * 2 * D], F16)
            st["maskrow"] = sb(c12, "maskrow", [1, B * KEYS], BF16)
            stage(st, latents)
            stage(st, cross0)
        stage(st, middle)
        stage(st, cross1)
        st["XR"] = sb(ctx, "XR", [P, NT, 2, D], F16)
        stage(st, poly)
        stage(st, experts)


def load_weights(st, c, block, tag, first, cols, dst, base=0):
    nc, sig, d = st["nc"], st["sig"], st["d"]
    ring = [st["sb"](c, f"{tag}_stage{i}", [P, STAGE]) for i in range(2)]
    pieces = [(a, min(STAGE, cols - a)) for a in range(0, cols, STAGE)]
    came = [sig[f"{tag}_came{i}"] for i in range(2)]
    hi_done, lo_done = sig[f"{tag}_hi"], sig[f"{tag}_lo"]

    def sync(sp):
        for n, (a, w) in enumerate(pieces):
            if n >= 2:
                sp.wait_ge(lo_done, n - 1)
            sp.dma_start(ring[n % 2][:, 0:w], d["W"][:, first + a:first + a + w]).then_inc(came[n % 2], 16)

    def scalar(act):
        for n, (a, w) in enumerate(pieces):
            act.wait_ge(came[n % 2], 16 * (n // 2 + 1))
            act.activation(dst[:, 0, base + a:base + a + w], ring[n % 2][:, 0:w], ACT.Copy, scale=WS).then_inc(hi_done, 1)

    def vector(dve):
        for n, (a, w) in enumerate(pieces):
            dve.wait_ge(came[n % 2], 16 * (n // 2 + 1))
            dve.wait_ge(hi_done, n + 1)
            dve.scalar_tensor_tensor(dst[:, 1, base + a:base + a + w], ring[n % 2][:, 0:w], WS,
                                     dst[:, 0, base + a:base + a + w], ALU.mult, ALU.subtract).then_inc(lo_done, 1)

    return sync, scalar, vector, (lo_done, len(pieces))


def latents(st):
    nc, d, sig, sb = st["nc"], st["d"], st["sig"], st["sb"]
    X, XT, KL, KR, K1R = st["X"], st["XT"], st["KL"], st["KR"], st["K1R"]
    vecs, vecs16, ident, mhalf = st["vecs"], st["vecs16"], st["ident"], st["mhalf"]
    with ExitStack() as c:
        W = sb(c, "W1", [P, 2, CK * 3 * D], F16)
        W12 = st["W12"]
        mask8 = sb(c, "mask8", [1, B, SC], U8)
        z = [sb(c, f"z{u}", [P, CK * P]) for u in range(2)]
        y1 = [sb(c, f"y1_{u}", [P, D]) for u in range(2)]
        y2 = [sb(c, f"y2_{u}", [P, D]) for u in range(2)]
        LT = [sb(c, f"LT{u}", [P, 2, CK, P], F16) for u in range(2)]
        sq = [sb(c, f"sq{i}", [P, D]) for i in range(2)]
        ss = [sb(c, f"ss{i}", [P, H0]) for i in range(2)]
        rn = [sb(c, f"rn{i}", [P, H0]) for i in range(2)]
        kh = [sb(c, f"kh{i}", [P, D]) for i in range(2)]
        vl = [sb(c, f"vl{u}", [P, 2, D], F16) for u in range(2)]
        rem = sb(c, "rem", [B, DC])
        remT = sb(c, "remT", [P, XK, B])
        remTh = sb(c, "remTh", [P, 2, XK, B], F16)
        W1R = sb(c, "W1R", [P, 2, 2 * XK * D], F16)
        pT = [c.enter_context(nc.psum_tensor(f"pT{u}", [P, D], F32)) for u in range(2)]
        pQ, pK, pV = (c.enter_context(nc.psum_tensor(n, [P, D], F32)) for n in ("pQ", "pK", "pV"))
        pH = [c.enter_context(nc.psum_tensor(f"pH{i}", [P, D], F32)) for i in range(2)]
        block = c.enter_context(nc.Block())
        kvc = c.enter_context(ExitStack())
        first = load_weights(st, kvc, block, "wlat", WAT["q0"], CK * 3 * D, W)
        second = load_weights(st, kvc, block, "wctx", WAT["kv0"], XK * 2 * D, W12)
        third = load_weights(st, kvc, block, "wrem", WAT["k1"], 2 * XK * D, W1R)
        ln1, ln2 = Norm(sig, "lat1", st["work"]), Norm(sig, "lat2", st["work"])
        lnr = Norm(sig, "rem", st["work"])
        pair = lambda t, *ix: (t[(slice(None), 0, *ix)], t[(slice(None), 1, *ix)])

        @block.sync
        def _(sp):
            sig.begin(sp, "vlat_out0", "vlat_out1")
            sp.dma_start(X[:, :, :], d["x"].rearrange("(t p) n -> p t n", p=P)).then_inc(sig["x_in"], 16)
            sp.dma_start(vecs[:, :], d["vecs"]).then_inc(sig["small_in"], 16)
            sp.dma_start(rem[:, :], d["rem"]).then_inc(sig["small_in"], 16)
            sp.dma_start(remT[:, :, :], d["remT"]).then_inc(sig["small_in"], 16)
            sp.dma_start(mask8[:, :, :], d["mask"]).then_inc(sig["small_in"], 16)
            first[0](sp)
            second[0](sp)
            third[0](sp)
            with sp.Fori(0, NT // 2) as pair_no:
                t0 = pair_no * 2
                for u in range(2):
                    t = t0 + u
                    sp.wait_ge(sig["vl_lo"], t + 1 + STARTS["vl_lo"])
                    sp.dma_start(st["vlat"][ds(t * P, P), :], vl[u][:, :, :].rearrange("p a n -> p (a n)"))\
                      .then_inc(sig[f"vlat_out{u}"], 16)
            sp.wait_ge(sig["vl_lo"], NT + 1 + STARTS["vl_lo"])
            sp.dma_start(st["vrem"], vl[0][0:B, :, :].rearrange("p a n -> p (a n)")).then_inc(sig["vrem_out"], 16)
            sp.wait_ge(sig["vl_lo"], NT + 2 + STARTS["vl_lo"])
            sp.dma_start(st["vrem1"], vl[1][0:B, :, :].rearrange("p a n -> p (a n)")).then_inc(sig["vrem_out"], 16)
            for u in range(2):
                sp.wait_ge(sig[f"vlat_out{u}"], 16 * (NT // 2) + STARTS[f"vlat_out{u}"])
            sp.wait_ge(sig["vrem_out"], 32)

        @block.gpsimd
        def _(pool):
            pool.memset(ident[:, :], 0.0).then_inc(sig["consts"], 1)
            pool.memset(mhalf[:, :], -0.5).then_inc(sig["consts"], 1)
            pool.memset(st["maskrow"][:, :], 0.0).then_inc(sig["consts"], 1)
            pool.wait_ge(sig["consts"], 3)
            pool.affine_select(out=ident[:, :], in_=ident[:, :], compare_op=ALU.not_equal, fill=1.0, base=0,
                               pattern=[[-1, P]], channel_multiplier=1).then_inc(sig["consts"], 1)
            pool.wait_ge(sig["small_in"], 64)
            pool.tensor_scalar(vecs16[:, :], vecs[:, :], WS, None, ALU.mult).then_inc(sig["consts"], 1)
            rows = st["maskrow"][:, :].rearrange("p (b k) -> p b k", b=B)
            pool.tensor_scalar(rows[:, :, 0:FULL], mask8[:, :, 0:FULL], 1.0, -MASKED, ALU.subtract, ALU.mult).then_inc(sig["consts"], 1)
            pool.tensor_scalar(rows[:, :, KEYS - 1:KEYS], mask8[:, :, FULL:SC], 1.0, -MASKED, ALU.subtract, ALU.mult).then_inc(sig["consts"], 1)

            def rms_power(n, i, rows):
                pool.wait_ge(sig[f"ss{i}"], n + 1)
                sig.passed(pool, "pool")
                a, r = ss[i][0:rows, :], rn[i][0:rows, :]
                pool.tensor_scalar(a, a, 1.0 / (HD0 * WS * WS), 1e-16, ALU.mult, ALU.max).then_inc(sig[f"ms{i}"], 1)
                pool.wait_ge(sig[f"ms{i}"], n + 1)
                pool.tensor_tensor(r, a, mhalf[0:rows, 0:H0], ALU.pow).then_inc(sig[f"rn{i}"], 1)

            with pool.Fori(0, NT // 2) as pair_no:
                t0 = pair_no * 2
                for u in range(2):
                    ln1.power(pool, u, t0 + u, mhalf)
                for u in range(2):
                    ln2.power(pool, u, t0 + u, mhalf)
                for u in range(2):
                    rms_power(t0 + u, 0, P)
                    rms_power(t0 + u, 1, P)
            lnr.power(pool, 0, 0, mhalf, B)
            rms_power(NT, 1, B)

        def rms_scale(dve, n, i, src, rows):
            dve.wait_ge(sig[f"rn{i}"], n + 1)
            dve.scalar_tensor_tensor(kh[i][0:rows, :].rearrange("p (h d) -> p h d", d=HD0),
                                     src[0:rows, :].rearrange("p (h d) -> p h d", d=HD0), 1.0 / WS,
                                     rn[i][0:rows, :].unsqueeze(2).broadcast_to([rows, H0, HD0]), ALU.mult, ALU.mult)\
               .then_inc(sig[f"kh{i}"], 1)

        def squares(dve, n, i, rows):
            dve.wait_ge(sig[f"sq{i}"], n + 1)
            dve.tensor_reduce(ss[i][0:rows, :], sq[i][0:rows, :].rearrange("p (h d) -> p h d", d=HD0), AX.X, ALU.add)\
               .then_inc(sig[f"ss{i}"], 1)

        @block.vector
        def _(dve):
            sig.begin(dve, "kh0", "kh1", "vl_lo", "hT0_lo", "hT1_lo")
            dve.wait_ge(sig["x_in"], 16)
            first[2](dve)
            second[2](dve)
            third[2](dve)
            dve.wait_ge(sig["small_in"], 64)
            dve.wait_ge(sig["consts"], 7)
            with dve.Fori(0, NT // 2) as pair_no:
                t0 = pair_no * 2
                xt = lambda u: X[:, ds(t0 + u, 1), :].rearrange("p a n -> p (a n)")
                for u in range(2):
                    ln1.stats(dve, u, t0 + u, xt(u))
                for u in range(2):
                    ln1.scale(dve, u, t0 + u, xt(u), y1[u][:, :])
                    dve.wait_ge(ln1.done, t0 + u + 1)
                    ln2.stats(dve, u, t0 + u, y1[u][:, :])
                for u in range(2):
                    ln2.scale(dve, u, t0 + u, y1[u][:, :], y2[u][:, :])
                for u in range(2):
                    t = t0 + u
                    dve.wait_ge(sig["latT"], t + 1)
                    for k in range(CK):
                        i = dve.tensor_scalar(z[u][:, k * P:(k + 1) * P], pT[u][:, k * P:(k + 1) * P],
                                              vecs[:, VAT["lng"] + k:VAT["lng"] + k + 1],
                                              vecs[:, VAT["lnb"] + k:VAT["lnb"] + k + 1], ALU.mult, ALU.add)
                        i.then_inc(sig["lat_z"], 1)
                    dve.wait_ge(sig["lat_hi"], t + 1)
                    dve.tensor_tensor(LT[u][:, 1, :, :], z[u][:, :].rearrange("p (k n) -> p k n", k=CK),
                                      LT[u][:, 0, :, :], ALU.subtract).then_inc(sig["lat_lo"], 1)
                for u in range(2):
                    t = t0 + u
                    squares(dve, t, 0, P)
                    squares(dve, t, 1, P)
                    rms_scale(dve, t, 0, pQ, P)
                    rms_scale(dve, t, 1, pK, P)
                    dve.wait_ge(sig["vl_hi"], t + 1)
                    dve.scalar_tensor_tensor(vl[u][:, 1, :], pV[:, :], 1.0 / WS, vl[u][:, 0, :], ALU.mult, ALU.subtract)\
                       .then_inc(sig["vl_lo"], 1)
                    for i, dst, g in ((0, XT, "qg"), (1, KL, "kg")):
                        dve.wait_ge(sig[f"hT{i}_hi"], t + 1)
                        dve.scalar_tensor_tensor(dst[:, 1, :, ds(t * P, P)], pH[i][:, :].rearrange("p (k n) -> p k n", k=CK),
                                                 vecs[:, VAT[g]:VAT[g] + 1], dst[:, 0, :, ds(t * P, P)],
                                                 ALU.mult, ALU.subtract).then_inc(sig[f"hT{i}_lo"], 1)
            lnr.stats(dve, 0, 0, rem[:, :], B)
            lnr.scale(dve, 0, 0, rem[:, :], y1[0][0:B, 0:DC], B)
            dve.wait_ge(sig["latT"], NT + 1)
            for k in range(XK):
                dve.tensor_scalar(z[0][:, k * B:(k + 1) * B], pT[0][:, k * B:(k + 1) * B],
                                  vecs[:, VAT["lxg"] + k:VAT["lxg"] + k + 1],
                                  vecs[:, VAT["lxb"] + k:VAT["lxb"] + k + 1], ALU.mult, ALU.add).then_inc(sig["lat_z"], 1)
            dve.wait_ge(sig["lat_hi"], NT + 1)
            dve.tensor_tensor(LT[0][:, 1, 0:XK, 0:B], z[0][:, 0:XK * B].rearrange("p (k n) -> p k n", k=XK),
                              LT[0][:, 0, 0:XK, 0:B], ALU.subtract).then_inc(sig["lat_lo"], 1)
            dve.wait_ge(sig["lat_hi"], NT + 2)
            dve.tensor_tensor(remTh[:, 1, :, :], remT[:, :, :], remTh[:, 0, :, :], ALU.subtract).then_inc(sig["lat_lo"], 1)
            squares(dve, NT, 1, B)
            rms_scale(dve, NT, 1, pK, B)
            dve.wait_ge(sig["vl_hi"], NT + 1)
            dve.scalar_tensor_tensor(vl[0][0:B, 1, :], pV[0:B, :], 1.0 / WS, vl[0][0:B, 0, :], ALU.mult, ALU.subtract)\
               .then_inc(sig["vl_lo"], 1)
            dve.wait_ge(sig["hT1_hi"], NT + 1)
            dve.scalar_tensor_tensor(KR[:, 1, :, :], pH[1][:, 0:CK * B].rearrange("p (k n) -> p k n", k=CK),
                                     vecs[:, VAT["kg"]:VAT["kg"] + 1], KR[:, 0, :, :], ALU.mult, ALU.subtract)\
               .then_inc(sig["hT1_lo"], 1)
            dve.wait_ge(sig["vl_hi"], NT + 2)
            dve.scalar_tensor_tensor(vl[1][0:B, 1, :], pQ[0:B, :], 1.0 / WS, vl[1][0:B, 0, :], ALU.mult, ALU.subtract)\
               .then_inc(sig["vl_lo"], 1)
            for k in range(CK):
                dve.wait_ge(sig["k1r_hi"], CK)
                dve.scalar_tensor_tensor(K1R[:, 1, k, :], pH[0][:, k * B:(k + 1) * B],
                                         vecs16[:, VAT["bk1"] + k:VAT["bk1"] + k + 1], K1R[:, 0, k, :],
                                         ALU.add, ALU.subtract).then_inc(sig["k1r_lo"], 1)

        @block.scalar
        def _(act):
            first[1](act)
            second[1](act)
            third[1](act)
            act.wait_ge(sig["small_in"], 64)
            act.wait_ge(sig["consts"], 7)
            with act.Fori(0, NT // 2) as pair_no:
                t0 = pair_no * 2
                for u in range(2):
                    t = t0 + u
                    act.wait_ge(sig["lat_z"], CK * t + CK)
                    act.activation(LT[u][:, 0, :, :], z[u][:, :].rearrange("p (k n) -> p k n", k=CK), ACT.Copy)\
                       .then_inc(sig["lat_hi"], 1)
                for u in range(2):
                    t = t0 + u
                    act.wait_ge(sig["lat_qkv"], t + 1)
                    act.activation(sq[0][:, :], pQ[:, :], ACT.Square).then_inc(sig["sq0"], 1)
                    act.activation(sq[1][:, :], pK[:, :], ACT.Square).then_inc(sig["sq1"], 1)
                    act.wait_ge(sig[f"vlat_out{u}"], t0 * 8 + STARTS[f"vlat_out{u}"])
                    act.activation(vl[u][:, 0, :], pV[:, :], ACT.Copy, scale=1.0 / WS)\
                       .then_inc(sig["vl_hi"], 1)
                    for i, dst, g in ((0, XT, "qg"), (1, KL, "kg")):
                        act.wait_ge(sig[f"hT{i}"], t + 1)
                        act.activation(dst[:, 0, :, ds(t * P, P)], pH[i][:, :].rearrange("p (k n) -> p k n", k=CK),
                                       ACT.Copy, scale=vecs[:, VAT[g]:VAT[g] + 1]).then_inc(sig[f"hT{i}_hi"], 1)
            act.wait_ge(sig["lat_z"], CK * NT + XK)
            act.activation(LT[0][:, 0, 0:XK, 0:B], z[0][:, 0:XK * B].rearrange("p (k n) -> p k n", k=XK), ACT.Copy)\
               .then_inc(sig["lat_hi"], 1)
            act.activation(remTh[:, 0, :, :], remT[:, :, :], ACT.Copy).then_inc(sig["lat_hi"], 1)
            act.wait_ge(sig["lat_qkv"], NT + 1)
            act.activation(sq[1][0:B, :], pK[0:B, :], ACT.Square).then_inc(sig["sq1"], 1)
            act.wait_ge(sig["vlat_out0"], 16 * (NT // 2) + STARTS["vlat_out0"])
            act.activation(vl[0][0:B, 0, :], pV[0:B, :], ACT.Copy, scale=1.0 / WS).then_inc(sig["vl_hi"], 1)
            act.wait_ge(sig["hT1"], NT + 1)
            act.activation(KR[:, 0, :, :], pH[1][:, 0:CK * B].rearrange("p (k n) -> p k n", k=CK), ACT.Copy,
                           scale=vecs[:, VAT["kg"]:VAT["kg"] + 1]).then_inc(sig["hT1_hi"], 1)
            act.wait_ge(sig["lat_qkv"], NT + 2)
            act.wait_ge(sig["vlat_out1"], 16 * (NT // 2) + STARTS["vlat_out1"])
            act.activation(vl[1][0:B, 0, :], pQ[0:B, :], ACT.Copy, scale=1.0 / WS).then_inc(sig["vl_hi"], 1)
            for k in range(CK):
                act.activation(K1R[:, 0, k, :], pH[0][:, k * B:(k + 1) * B], ACT.Identity,
                               bias=vecs16[:, VAT["bk1"] + k:VAT["bk1"] + k + 1]).then_inc(sig["k1r_hi"], 1)

        @block.tensor
        def _(pe):
            pe.wait_ge(sig["consts"], 7)
            pe.wait_ge(*first[3])
            Wq = W[:, :, 0:CK * D].rearrange("p a (k n) -> p a k n", k=CK)
            Wkv = W[:, :, CK * D:].rearrange("p a (k n) -> p a k n", k=CK)
            with pe.Fori(0, NT // 2) as pair_no:
                t0 = pair_no * 2
                for u in range(2):
                    t = t0 + u
                    pe.wait_ge(ln2.done, t + 1)
                    for k in range(CK):
                        i = pe.transpose(pT[u][:, k * P:(k + 1) * P], y2[u][:, k * P:(k + 1) * P], ident[:, :])
                    i.then_inc(sig["latT"], 1)
                for u in range(2):
                    t = t0 + u
                    pe.wait_ge(sig["lat_lo"], t + 1)
                    pe.wait_ge(sig["kh0"], t + STARTS["kh0"])
                    pe.wait_ge(sig["kh1"], t + STARTS["kh1"])
                    pe.wait_ge(sig["vl_lo"], t + STARTS["vl_lo"])
                    for out_, w, at in ((pQ, Wq, 0), (pK, Wkv, 0), (pV, Wkv, D)):
                        for k in range(CK):
                            i = product(pe, out_[:, :], pair(LT[u], k), pair(w, k, slice(at, at + D)), k == 0, k == CK - 1)
                    i.then_inc(sig["lat_qkv"], 1)
                    for j in range(2):
                        pe.wait_ge(sig[f"kh{j}"], t + 1 + STARTS[f"kh{j}"])
                        pe.wait_ge(sig[f"hT{j}_lo"], t + STARTS[f"hT{j}_lo"])
                        for k in range(CK):
                            i = pe.transpose(pH[j][:, k * P:(k + 1) * P], kh[j][:, k * P:(k + 1) * P], ident[:, :])
                        i.then_inc(sig[f"hT{j}"], 1)
            pe.wait_ge(lnr.done, 1)
            for k in range(XK):
                i = pe.transpose(pT[0][:, k * B:(k + 1) * B], y1[0][0:B, k * P:(k + 1) * P], ident[0:B, 0:B])
            i.then_inc(sig["latT"], 1)
            pe.wait_ge(*second[3])
            pe.wait_ge(sig["lat_lo"], NT + 2)
            pe.wait_ge(sig["kh1"], NT + STARTS["kh1"])
            pe.wait_ge(sig["vl_lo"], NT + STARTS["vl_lo"])
            Wx = W12[:, :, :].rearrange("p a (k n) -> p a k n", k=XK)
            for out_, at in ((pK, 0), (pV, D)):
                for k in range(XK):
                    i = product(pe, out_[0:B, :], pair(LT[0], k, slice(0, B)), pair(Wx, k, slice(at, at + D)), k == 0, k == XK - 1)
            i.then_inc(sig["lat_qkv"], 1)
            pe.wait_ge(*third[3])
            Wr = W1R[:, :, :].rearrange("p a (j k n) -> p a j k n", j=2, k=XK)
            pe.wait_ge(sig["kh0"], NT + STARTS["kh0"])
            pe.wait_ge(sig["hT0_lo"], NT + STARTS["hT0_lo"])
            for m in range(CK):
                for k in range(XK):
                    product(pe, pH[0][:, m * B:(m + 1) * B], pair(Wr, 0, k, slice(m * P, (m + 1) * P)),
                            pair(remTh, k), k == 0, k == XK - 1)
            for k in range(XK):
                i = product(pe, pQ[0:B, :], pair(remTh, k), pair(Wr, 1, k), k == 0, k == XK - 1)
            i.then_inc(sig["lat_qkv"], 1)
            pe.wait_ge(sig["kh1"], NT + 1 + STARTS["kh1"])
            pe.wait_ge(sig["hT1_lo"], NT + STARTS["hT1_lo"])
            for k in range(CK):
                i = pe.transpose(pH[1][:, k * B:(k + 1) * B], kh[1][0:B, k * P:(k + 1) * P], ident[0:B, 0:B])
            i.then_inc(sig["hT1"], 1)


def cross0(st):
    nc, d, sig, sb = st["nc"], st["d"], st["sig"], st["sb"]
    XT, KL, KR, vecs, ident, mhalf = st["XT"], st["KL"], st["KR"], st["vecs"], st["ident"], st["mhalf"]
    W = st["W12"][:, :, :].rearrange("p a (k n) -> p a k n", k=XK)
    SCALE = HD0 ** -0.5
    with ExitStack() as c:
        cx = [sb(c, f"cx{u}", [P, 2, DC]) for u in range(2)]
        v3 = [sb(c, f"v3_{u}", [S + 1, 2, D], F16) for u in range(2)]
        y = [sb(c, f"cy{u}", [P, 2, DC]) for u in range(2)]
        z = sb(c, "cz", [P, XK, FULL])
        LT = [sb(c, f"cLT{u}", [P, 2, XK, FULL], F16) for u in range(2)]
        sq, ss, rn, kh = sb(c, "csq", [P, D]), sb(c, "css", [P, H0]), sb(c, "crn", [P, H0]), sb(c, "ckh", [P, D])
        khat = [sb(c, f"khat{u}", [P, 2, CK, KEYS], F16) for u in range(2)]
        vb = [sb(c, f"vb{u}", [P, 2, 2, D], F16) for u in range(2)]
        qbd = [sb(c, f"qbd{u}", [P, 2, CK, P], F16) for u in range(2)]
        pr = sb(c, "probs", [P, 2, KEYS])
        mx, nm, rsum, rinv = (sb(c, n, [P, 2]) for n in ("cmx", "cnm", "crsum", "crinv"))
        PT = sb(c, "cPT", [P, 2, 2, 2, P], F16)
        PTt = sb(c, "cPTt", [S + 1, 2, 2, P], F16)
        ones = sb(c, "cones", [1, P], BF16)
        ps = lambda n, s: c.enter_context(nc.psum_tensor(n, s, F32))
        pT, pK, pV, pKT, pP, pO = (ps(n, [P, D]) for n in ("cpT", "cpK", "cpV", "cpKT", "cpP", "cpO"))
        pS = ps("cpS", [P, 2, 512])
        block = c.enter_context(nc.Block())
        ln = Norm(sig, "c0", st["work"])
        maskrow = st["maskrow"]

        def walk(eng, body, before=None, after=None):
            if before:
                before()
            body(0, 0, False, True)
            with eng.Fori(0, (B - 2) // 2) as i:
                body(i * 2 + 1, 1, True, True)
                body(i * 2 + 2, 0, True, True)
            body(B - 1, 1, True, False)
            if after:
                after()

        @block.sync
        def _(sp):
            def load(b, u, wait):
                if wait:
                    sp.wait_ge(sig["c0_norm"], 2 * b - 2)
                sp.dma_start(cx[u][:, :, :], d["ctx"][ds(b, 1), 0:FULL, :].rearrange("a (i p) n -> p (a i) n", p=P))\
                  .then_inc(sig[f"cx_in{u}"], 16)
                if wait:
                    sp.wait_ge(sig["c0_o"], b - 1)
                sp.dma_start(v3[u][0:S, :, :], st["vlat"][ds(b * S, S), :].rearrange("p (a n) -> p a n", a=2))\
                  .then_inc(sig[f"v3_in{u}"], 16)
                sp.dma_start(v3[u][S:S + 1, :, :], st["vrem"][ds(b, 1), :].rearrange("p (a n) -> p a n", a=2))\
                  .then_inc(sig[f"v3_in{u}"], 16)

            load(0, 0, False)
            load(1, 1, False)
            with sp.Fori(0, (B - 2) // 2) as i:
                load(i * 2 + 2, 0, True)
                load(i * 2 + 3, 1, True)

        @block.gpsimd
        def _(pool):
            sig.begin(pool, "c0_zlo")
            pool.memset(ones[:, :], 1.0).then_inc(sig["c0_const"], 1)
            for u in range(2):
                pool.memset(qbd[u][:, :, :, :], 0.0).then_inc(sig["c0_const"], 1)

            def low(b, u):
                pool.wait_ge(sig["c0_zhi"], b + 1)
                pool.tensor_tensor(LT[u][:, 1, :, :], z[:, :, :], LT[u][:, 0, :, :], ALU.subtract).then_inc(sig["c0_zlo"], 1)

            def rms(q):
                pool.wait_ge(sig["c0_ss"], q + 1 + STARTS["c0_ss"])
                sig.passed(pool, "pool")
                pool.tensor_scalar(ss[:, :], ss[:, :], 1.0 / (HD0 * WS * WS), 1e-16, ALU.mult, ALU.max).then_inc(sig["c0_ms"], 1)
                pool.wait_ge(sig["c0_ms"], q + 1)
                pool.tensor_tensor(rn[:, :], ss[:, :], mhalf[:, 0:H0], ALU.pow).then_inc(sig["c0_rn"], 1)

            def before():
                for i in range(2):
                    ln.power(pool, i, i, mhalf)
                low(0, 0)

            def body(b, u, prev, nxt):
                if nxt:
                    for i in range(2):
                        ln.power(pool, i, 2 * b + 2 + i, mhalf)
                rms(2 * b)
                rms(2 * b + 1)
                if nxt:
                    low(b + 1, 1 - u)

            walk(pool, body, before)

        @block.vector
        def _(dve):
            sig.begin(dve, "c0_kh", "c0_vlo", "c0_ktlo", "c0_ss", "c0_olo")

            def norm(b, u):
                for i in range(2):
                    if i == 0:
                        dve.wait_ge(sig[f"cx_in{u}"], 8 * b + (16 - 8 * u))
                    ln.stats(dve, i, 2 * b + i, cx[u][:, i, :])
                for i in range(2):
                    ln.scale(dve, i, 2 * b + i, cx[u][:, i, :], y[u][:, i, :])

            def high(b, u):
                dve.wait_ge(sig["c0_z"], XK * b + XK + STARTS["c0_z"])
                dve.tensor_copy(LT[u][:, 0, :, :], z[:, :, :]).then_inc(sig["c0_zhi"], 1)

            def key(q):
                dve.wait_ge(sig["c0_sq"], q + 1)
                dve.tensor_reduce(ss[:, :], sq[:, :].rearrange("p (h d) -> p h d", d=HD0), AX.X, ALU.add).then_inc(sig["c0_ss"], 1)

            def key_scale(q):
                dve.wait_ge(sig["c0_rn"], q + 1)
                dve.wait_ge(sig["c0_kt"], q + STARTS["c0_kt"])
                dve.scalar_tensor_tensor(kh[:, :].rearrange("p (h d) -> p h d", d=HD0),
                                         pK[:, :].rearrange("p (h d) -> p h d", d=HD0), 1.0 / WS,
                                         rn[:, :].unsqueeze(2).broadcast_to([P, H0, HD0]), ALU.mult, ALU.mult)\
                   .then_inc(sig["c0_kh"], 1)

            def value_low(q, u, i):
                dve.wait_ge(sig["c0_vhi"], q + 1)
                dve.scalar_tensor_tensor(vb[u][:, i, 1, :], pV[:, :], 1.0 / WS, vb[u][:, i, 0, :], ALU.mult, ALU.subtract)\
                   .then_inc(sig["c0_vlo"], 1)

            def key_low(q, u, i):
                dve.wait_ge(sig["c0_kthi"], q + 1)
                cols = slice(i * P, (i + 1) * P)
                dve.scalar_tensor_tensor(khat[u][:, 1, :, cols], pKT[:, :].rearrange("p (k n) -> p k n", k=CK),
                                         vecs[:, VAT["kg"]:VAT["kg"] + 1], khat[u][:, 0, :, cols], ALU.mult, ALU.subtract)\
                   .then_inc(sig["c0_ktlo"], 1)

            def gather(b, u):
                dve.tensor_copy(khat[u][:, :, :, FULL:FULL + S], KL[:, :, :, ds(b * S, S)]).then_inc(sig["c0_side"], 1)
                dve.tensor_copy(khat[u][:, :, :, KEYS - 1:KEYS], KR[:, :, :, ds(b, 1)]).then_inc(sig["c0_side"], 1)
                for j in range(2):
                    for k in range(2):
                        at = (2 * k + j) * S
                        dve.tensor_copy(qbd[u][j * HD0:(j + 1) * HD0, :, k::2, at:at + S],
                                        XT[j * HD0:(j + 1) * HD0, :, k::2, ds(b * S, S)]).then_inc(sig["c0_side"], 1)

            def softmax_max(b):
                dve.wait_ge(sig["c0_s"], b + 1)
                dve.tensor_reduce(mx[:, :], pS[:, :, 0:KEYS], AX.X, ALU.max).then_inc(sig["c0_mx"], 1)
                dve.wait_ge(sig["c0_mx"], b + 1)
                dve.tensor_scalar(nm[:, :], mx[:, :], -SCALE, None, ALU.mult).then_inc(sig["c0_nm"], 1)

            def softmax_scale(b):
                dve.wait_ge(sig["c0_exp"], 2 * b + 2 + STARTS["c0_exp"])
                dve.reciprocal(rinv[:, :], rsum[:, :]).then_inc(sig["c0_rinv"], 1)
                dve.wait_ge(sig["c0_rinv"], b + 1)
                for g in range(2):
                    dve.tensor_scalar(pr[:, g, :], pr[:, g, :], rinv[:, g:g + 1], None, ALU.mult).then_inc(sig["c0_pr"], 1)

            def probs_low(b):
                dve.wait_ge(sig["c0_pthi"], 2 * b + 2)
                dve.tensor_tensor(PT[:, 1, :, :, :].rearrange("p g i n -> p (g i n)"), pP[:, :],
                                  PT[:, 0, :, :, :].rearrange("p g i n -> p (g i n)"), ALU.subtract).then_inc(sig["c0_ptlo"], 1)
                dve.tensor_tensor(PTt[:, 1, :, :].rearrange("p g n -> p (g n)"), pO[0:S + 1, 0:2 * P],
                                  PTt[:, 0, :, :].rearrange("p g n -> p (g n)"), ALU.subtract).then_inc(sig["c0_ptlo"], 1)

            def out_low(b):
                dve.wait_ge(sig["c0_ohi"], 2 * b + 2)
                o = pO[:, 256:512].rearrange("p (k n) -> p k n", k=CK)
                for j in range(2):
                    rows = slice(j * HD0, (j + 1) * HD0)
                    dve.tensor_tensor(XT[rows, 1, :, ds(b * S, S)], o[rows, :, j * S:(j + 1) * S],
                                      XT[rows, 0, :, ds(b * S, S)], ALU.subtract).then_inc(sig["c0_olo"], 1)

            def before():
                norm(0, 0)
                high(0, 0)

            def body(b, u, prev, nxt):
                if nxt:
                    norm(b + 1, 1 - u)
                key(2 * b)
                key_scale(2 * b)
                value_low(2 * b, u, 0)
                if prev:
                    softmax_max(b - 1)
                gather(b, u)
                if prev:
                    softmax_scale(b - 1)
                key(2 * b + 1)
                key_low(2 * b, u, 0)
                key_scale(2 * b + 1)
                if nxt:
                    high(b + 1, 1 - u)
                value_low(2 * b + 1, u, 1)
                if prev:
                    probs_low(b - 1)
                key_low(2 * b + 1, u, 1)
                if prev:
                    out_low(b - 1)

            def after():
                softmax_max(B - 1)
                softmax_scale(B - 1)
                probs_low(B - 1)
                out_low(B - 1)

            dve.wait_ge(sig["c0_const"], 3)
            walk(dve, body, before, after)

        @block.scalar
        def _(act):
            sig.begin(act, "c0_exp", "c0_z")

            def affine(b):
                act.wait_ge(sig["c0_zlo"], b + STARTS["c0_zlo"])
                for k in range(XK):
                    if k == 0:
                        act.wait_ge(sig["c0_T"], b + 1)
                    src = pT[:, k * FULL:(k + 1) * FULL] if k < 2 else pP[:, 0:FULL]
                    act.activation(z[:, k, :], src, ACT.Identity, bias=vecs[:, VAT["lxb"] + k:VAT["lxb"] + k + 1],
                                   scale=vecs[:, VAT["lxg"] + k:VAT["lxg"] + k + 1]).then_inc(sig["c0_z"], 1)

            def square(q):
                act.wait_ge(sig["c0_k"], q + 1)
                act.wait_ge(sig["c0_ss"], q + STARTS["c0_ss"])
                act.activation(sq[:, :], pK[:, :], ACT.Square).then_inc(sig["c0_sq"], 1)

            def value_high(q, u, i):
                act.wait_ge(sig["c0_v"], q + 1)
                act.activation(vb[u][:, i, 0, :], pV[:, :], ACT.Copy, scale=1.0 / WS).then_inc(sig["c0_vhi"], 1)

            def key_high(q, u, i):
                act.wait_ge(sig["c0_kt"], q + 1 + STARTS["c0_kt"])
                act.activation(khat[u][:, 0, :, i * P:(i + 1) * P], pKT[:, :].rearrange("p (k n) -> p k n", k=CK),
                               ACT.Copy, scale=vecs[:, VAT["kg"]:VAT["kg"] + 1]).then_inc(sig["c0_kthi"], 1)

            def exps(b):
                act.wait_ge(sig["c0_nm"], b + 1)
                act.wait_ge(sig["c0_pt"], b + STARTS["c0_pt"])
                for g in range(2):
                    act.activation(pr[:, g, :], pS[:, g, 0:KEYS], ACT.Exp, bias=nm[:, g:g + 1], scale=SCALE,
                                   accum_out=rsum[:, g:g + 1]).then_inc(sig["c0_exp"], 1)

            def probs_high(b):
                act.wait_ge(sig["c0_pt"], b + 1 + STARTS["c0_pt"])
                act.activation(PT[:, 0, :, :, :].rearrange("p g i n -> p (g i n)"), pP[:, :], ACT.Copy).then_inc(sig["c0_pthi"], 1)
                act.activation(PTt[:, 0, :, :].rearrange("p g n -> p (g n)"), pO[0:S + 1, 0:2 * P], ACT.Copy)\
                   .then_inc(sig["c0_pthi"], 1)

            def out_high(b):
                act.wait_ge(sig["c0_o"], b + 1)
                o = pO[:, 256:512].rearrange("p (k n) -> p k n", k=CK)
                for j in range(2):
                    rows = slice(j * HD0, (j + 1) * HD0)
                    act.activation(XT[rows, 0, :, ds(b * S, S)], o[rows, :, j * S:(j + 1) * S], ACT.Copy)\
                       .then_inc(sig["c0_ohi"], 1)

            def body(b, u, prev, nxt):
                square(2 * b)
                value_high(2 * b, u, 0)
                if prev:
                    exps(b - 1)
                square(2 * b + 1)
                key_high(2 * b, u, 0)
                if nxt:
                    affine(b + 1)
                value_high(2 * b + 1, u, 1)
                if prev:
                    probs_high(b - 1)
                key_high(2 * b + 1, u, 1)
                if prev:
                    out_high(b - 1)

            def after():
                exps(B - 1)
                probs_high(B - 1)
                out_high(B - 1)

            def before():
                affine(0)

            walk(act, body, before, after)

        @block.tensor
        def _(pe):
            sig.begin(pe, "c0_kt", "c0_pt")
            hl = lambda t, *ix: (t[(slice(None), 0, *ix)], t[(slice(None), 1, *ix)])

            def turn_context(b, u):
                for i in range(2):
                    pe.wait_ge(ln.done, 2 * b + i + 1)
                    if i == 0:
                        pe.wait_ge(sig["c0_z"], XK * b + STARTS["c0_z"])
                    for k in range(XK):
                        dst = pT[:, k * FULL + i * P:k * FULL + (i + 1) * P] if k < 2 else pP[:, i * P:(i + 1) * P]
                        t = pe.transpose(dst, y[u][:, i, k * P:(k + 1) * P], ident[:, :])
                t.then_inc(sig["c0_T"], 1)

            def project(q, u, i, dst, at, free, made):
                pe.wait_ge(sig[free], q + STARTS[free])
                for k in range(XK):
                    m = product(pe, dst[:, :], hl(LT[u], k, slice(i * P, (i + 1) * P)), hl(W, k, slice(at, at + D)),
                                k == 0, k == XK - 1)
                m.then_inc(sig[made], 1)

            def turn_key(q):
                pe.wait_ge(sig["c0_kh"], q + 1 + STARTS["c0_kh"])
                pe.wait_ge(sig["c0_ktlo"], q + STARTS["c0_ktlo"])
                for k in range(CK):
                    t = pe.transpose(pKT[:, k * P:(k + 1) * P], kh[:, k * P:(k + 1) * P], ident[:, :])
                t.then_inc(sig["c0_kt"], 1)

            def scores(b, u):
                pe.wait_ge(sig["c0_exp"], 2 * b + STARTS["c0_exp"])
                pe.wait_ge(sig["c0_ktlo"], 2 * b + 2 + STARTS["c0_ktlo"])
                pe.wait_ge(sig["c0_side"], 6 * b + 6)
                for g in range(2):
                    pe.matmul(pS[:, g, 0:KEYS], ones[0:1, :], maskrow[0:1, ds(b * KEYS, KEYS)], start=True, stop=False)
                    for k in (2 * g, 2 * g + 1):
                        m = product(pe, pS[:, g, 0:KEYS], hl(qbd[u], k), hl(khat[u], k), False, k == 2 * g + 1)
                m.then_inc(sig["c0_s"], 1)

            def turn_probs(b):
                pe.wait_ge(sig["c0_pr"], 2 * b + 2)
                pe.wait_ge(sig["c0_olo"], 2 * b + STARTS["c0_olo"])
                pe.wait_ge(sig["c0_z"], (XK * min(b + 3, B) if isinstance(b, int) else XK * b + 3 * XK) + STARTS["c0_z"])
                for g in range(2):
                    for i in range(2):
                        pe.transpose(pP[:, (2 * g + i) * P:(2 * g + i + 1) * P], pr[:, g, i * P:(i + 1) * P], ident[:, :])
                    t = pe.transpose(pO[0:S + 1, g * P:(g + 1) * P], pr[:, g, FULL:KEYS], ident[:, :])
                t.then_inc(sig["c0_pt"], 1)

            def outputs(b, u):
                pe.wait_ge(sig["c0_ptlo"], 2 * b + 2)
                pe.wait_ge(sig["c0_vlo"], 2 * b + 2 + STARTS["c0_vlo"])
                pe.wait_ge(sig[f"v3_in{u}"], 16 * b + (32 - 16 * u))
                for k in range(CK):
                    g, h = k // 2, (2 * k) % 4
                    o = pO[:, 256 + k * 64:256 + (k + 1) * 64]
                    qs, fs = slice(h * S, (h + 2) * S), slice(k * P, (k + 1) * P)
                    for i in range(2):
                        product(pe, o, (vb[u][:, i, 0, fs], vb[u][:, i, 1, fs]),
                                (PT[:, 0, g, i, qs], PT[:, 1, g, i, qs]), i == 0, False)
                    m = product(pe, o, (v3[u][:, 0, fs], v3[u][:, 1, fs]), (PTt[:, 0, g, qs], PTt[:, 1, g, qs]), False, True)
                m.then_inc(sig["c0_o"], 1)

            def before():
                turn_context(0, 0)

            def body(b, u, prev, nxt):
                pe.wait_ge(sig["c0_zlo"], b + 1 + STARTS["c0_zlo"])
                project(2 * b, u, 0, pK, 0, "c0_kh", "c0_k")
                project(2 * b, u, 0, pV, D, "c0_vlo", "c0_v")
                if prev:
                    scores(b - 1, 1 - u)
                project(2 * b + 1, u, 1, pK, 0, "c0_kh", "c0_k")
                turn_key(2 * b)
                if nxt:
                    turn_context(b + 1, 1 - u)
                project(2 * b + 1, u, 1, pV, D, "c0_vlo", "c0_v")
                if prev:
                    turn_probs(b - 1)
                turn_key(2 * b + 1)
                if prev:
                    outputs(b - 1, 1 - u)

            def after():
                scores(B - 1, (B - 1) % 2)
                turn_probs(B - 1)
                outputs(B - 1, (B - 1) % 2)

            walk(pe, body, before, after)


def gates(sig, dve, name, n, lg, tri, w):
    gt, eq, rank, sel, mx, sh = w["gt"], w["eq"], w["rank"], w["sel"], w["mx"], w["sh"]
    m = lg.shape[1]
    other, own = lg.unsqueeze(2).broadcast_to([P, m, 8, 8]), lg.unsqueeze(3).broadcast_to([P, m, 8, 8])
    s = sig[name]
    base = n * 7
    dve.tensor_tensor(gt, other, own, ALU.is_gt).then_inc(s, 1)
    dve.tensor_tensor(eq, other, own, ALU.is_equal).then_inc(s, 1)
    dve.wait_ge(s, base + 2)
    dve.tensor_tensor(eq, eq, tri.unsqueeze(1).broadcast_to([P, m, 8, 8]), ALU.mult).then_inc(s, 1)
    dve.wait_ge(s, base + 3)
    dve.tensor_tensor(gt, gt, eq, ALU.add).then_inc(s, 1)
    dve.wait_ge(s, base + 4)
    dve.tensor_reduce(rank, gt, AX.X, ALU.add).then_inc(s, 1)
    dve.tensor_reduce(mx, lg, AX.X, ALU.max).then_inc(s, 1)
    dve.wait_ge(s, base + 6)
    dve.tensor_scalar(sel, rank, 2.0, None, ALU.is_lt).then_inc(s, 1)
    dve.tensor_tensor(sh, lg, mx.unsqueeze(2).broadcast_to([P, m, 8]), ALU.subtract).then_inc(sig[name + "_sh"], 1)


def gates_end(sig, dve, name, n, out, w):
    s = sig[name + "_end"]
    m = out.shape[1]
    dve.wait_ge(sig[name + "_ex"], n + 1)
    dve.wait_ge(sig[name], n * 7 + 7)
    dve.tensor_tensor(w["ex"], w["ex"], w["sel"], ALU.mult).then_inc(s, 1)
    dve.wait_ge(s, n * 3 + 1)
    dve.tensor_reduce(w["mx"], w["ex"], AX.X, ALU.add).then_inc(s, 1)
    dve.wait_ge(s, n * 3 + 2)
    dve.reciprocal(w["mx"], w["mx"]).then_inc(s, 1)
    dve.wait_ge(s, n * 3 + 3)
    dve.tensor_tensor(out, w["ex"], w["mx"].unsqueeze(2).broadcast_to([P, m, 8]), ALU.mult).then_inc(sig[name + "_gate"], 1)


def gate_work(sb, c, tag, m):
    g = lambda n, s: sb(c, f"{tag}_{n}", s)
    return {"gt": g("gt", [P, m, 8, 8])[:, :, :, :], "eq": g("eq", [P, m, 8, 8])[:, :, :, :],
            "rank": g("rank", [P, m, 8])[:, :, :], "sel": g("sel", [P, m, 8])[:, :, :],
            "sh": g("sh", [P, m, 8])[:, :, :], "ex": g("ex", [P, m, 8])[:, :, :], "mx": g("mx", [P, m])[:, :]}


def by_pairs(eng, stages):
    with eng.Fori(0, NT // 2) as i:
        for stage in stages:
            for u in range(2):
                stage(i * 2 + u, u)


class Turn:

    def __init__(self, sig, name, ready, y, bank, LT, ident):
        self.sig, self.n, self.ready, self.y, self.bank, self.LT, self.ident = sig, name, ready, y, bank, LT, ident

    def turn(self, pe):
        def f(t, u):
            pe.wait_ge(self.ready, t + 1)
            for k in range(CK):
                i = pe.transpose(self.bank[u][:, k * P:(k + 1) * P], self.y[u][:, k * P:(k + 1) * P], self.ident[:, :])
            i.then_inc(self.sig[self.n + "_T"], 1)
        return f

    def parts(self, t, u):
        dst = self.LT(t, u) if callable(self.LT) else self.LT[u][:, :, :, :]
        return self.bank[u][:, :].rearrange("p (k n) -> p k n", k=CK), dst[:, 0, :, :], dst[:, 1, :, :]

    def high(self, act):
        def f(t, u):
            src, hi, _ = self.parts(t, u)
            act.wait_ge(self.sig[self.n + "_T"], t + 1)
            act.activation(hi, src, ACT.Copy).then_inc(self.sig[self.n + "_hi"], 1)
        return f

    def low(self, dve):
        def f(t, u):
            src, hi, lo = self.parts(t, u)
            dve.wait_ge(self.sig[self.n + "_hi"], t + 1)
            dve.tensor_tensor(lo, src, hi, ALU.subtract).then_inc(self.sig[self.n + "_lo"], 1)
        return f


def middle(st):
    nc, d, sig, sb = st["nc"], st["d"], st["sig"], st["sb"]
    X, XT, vecs16, ident, mhalf = st["X"], st["XT"], st["vecs16"], st["ident"], st["mhalf"]
    with ExitStack() as c:
        cols = WAT["q1"] + CK * D - WAT["o0"]
        W = sb(c, "W3", [P, 2, cols], F16)
        w3 = lambda n, m, k=CK: W[:, :, WAT[n] - WAT["o0"]:WAT[n] - WAT["o0"] + k * m].rearrange("p a (k n) -> p a k n", k=k)
        Wo, Wqkv, Wd, Wu, Wr, Wq1 = w3("o0", D), w3("qkv0", 3 * D), w3("down", P), w3("up", D, 1), w3("r0", E0), w3("q1", D)
        two = lambda n, s, dt=F32: [sb(c, f"mid_{n}{u}", s, dt) for u in range(2)]
        rows = sb(c, "mrows", [P, 2, D])
        y, y2, zt = two("y", [P, D]), two("y2", [P, D]), two("zt", [P, D])
        LT = two("LT", [P, 2, CK, P], F16)
        qT, kT = two("qT", [P, 2, CK, P], F16), two("kT", [P, 2, CK, P], F16)
        v = two("v", [P, 2, D], F16)
        sc, ex, mx, rs = two("sc", [P, S]), two("ex", [P, S]), two("mx", [P, 2]), two("rs", [P, 2])
        aB = two("aB", [P, 2, P], F16)
        dg, dT = two("dg", [P, P]), two("dT", [P, 2, P], F16)
        lg, gate, gsel = two("lg", [P, 1, 8]), two("gate", [P, 1, 8]), two("gsel", [P, 8])
        work = [gate_work(sb, c, f"mg{u}", 1) for u in range(2)]
        tri, sel = sb(c, "mtri", [P, 8, 8]), sb(c, "msel", [P, P])
        bank = lambda n: [c.enter_context(nc.psum_tensor(f"mid_{n}{u}", [P, D], F32)) for u in range(2)]
        bT, bA, bB, bC = bank("T"), bank("A"), bank("B"), bank("C")
        block = c.enter_context(nc.Block())
        lc = c.enter_context(ExitStack())
        load = load_weights(st, lc, block, "w3", WAT["o0"], cols, W)
        na, nb, nq = (Norm(sig, f"m_{n}", st["work"]) for n in "abq")
        ta = Turn(sig, "m_ta", na.done, y, bT, LT, ident)
        tb = Turn(sig, "m_tb", nb.done, y2, bT, LT, ident)
        tq = Turn(sig, "m_tq", nq.done, y, bT, LT, ident)
        hl = lambda t, *ix: (t[(slice(None), 0, *ix)], t[(slice(None), 1, *ix)])
        tile = lambda t: X[:, ds(t, 1), :].rearrange("p a n -> p (a n)")
        bias = lambda n, k: vecs16[:, VAT[n] + k:VAT[n] + k + 1]

        @block.sync
        def _(sp):
            for i in range(2):
                sp.dma_start(rows[:, i, :], d["rows"][i:i + 1, :].broadcast_to([P, D])).then_inc(sig["m_rows"], 16)
            load[0](sp)

        @block.gpsimd
        def _(pool):
            pool.memset(tri[:, :, :], 1.0).then_inc(sig["m_const"], 1)
            pool.memset(sel[:, :], 0.0).then_inc(sig["m_const"], 1)
            for u in range(2):
                pool.memset(aB[u][:, :, :], 0.0).then_inc(sig["m_const"], 1)
            pool.wait_ge(sig["m_const"], 4)
            pool.affine_select(out=tri[:, :, :], in_=tri[:, :, :], compare_op=ALU.is_gt, fill=0.0, base=0,
                               pattern=[[1, 8], [-1, 8]], channel_multiplier=0).then_inc(sig["m_const"], 1)
            pool.affine_select(out=sel[:, :].rearrange("p (b s) -> p b s", b=BPT), in_=sel[:, :].rearrange("p (b s) -> p b s", b=BPT),
                               compare_op=ALU.not_equal, fill=1.0, base=0,
                               pattern=[[-S, BPT], [0, S]], channel_multiplier=1).then_inc(sig["m_const"], 1)
            by_pairs(pool, [lambda t, u, n=n: n.power(pool, u, t, mhalf) for n in (na, nb, nq)])

        @block.vector
        def _(dve):
            load[2](dve)
            dve.wait_ge(sig["m_const"], 6)
            dve.wait_ge(sig["m_rows"], 32)

            def residual_o(t, u):
                dve.tensor_tensor(tile(t), tile(t), rows[:, 0, :], ALU.add).then_inc(sig["m_xo"], 1)
                dve.wait_ge(sig["m_xo"], 2 * t + 1)
                dve.wait_ge(sig["m_o"], t + 1)
                dve.scalar_tensor_tensor(tile(t), bA[u][:, :], 1.0 / WS, tile(t), ALU.mult, ALU.add).then_inc(sig["m_xo"], 1)
                dve.wait_ge(sig["m_xo"], 2 * t + 2)
                sig.passed(dve, "dve")
                na.stats(dve, u, t, tile(t))

            def qk_low(t, u):
                for n, (dst, b, nm) in enumerate(((qT, bB, "m_q"), (kT, bC, "m_k"))):
                    dve.wait_ge(sig[nm + "_hi"], CK * t + CK)
                    for k in range(CK):
                        dve.scalar_tensor_tensor(dst[u][:, 1, k, :], b[u][:, k * P:(k + 1) * P], bias("bqk0", n * CK + k),
                                                 dst[u][:, 0, k, :], ALU.add, ALU.subtract).then_inc(sig[nm + "_lo"], 1)

            def value(t, u):
                dve.wait_ge(sig["m_v"], t + 1)
                dve.scalar_tensor_tensor(zt[u][:, :], bA[u][:, :], 1.0 / WS, rows[:, 1, :], ALU.mult, ALU.add).then_inc(sig["m_vz"], 1)

            def value_low(t, u):
                dve.wait_ge(sig["m_v_hi"], t + 1)
                dve.tensor_tensor(v[u][:, 1, :], zt[u][:, :], v[u][:, 0, :], ALU.subtract).then_inc(sig["m_v_lo"], 1)

            def soft(t, u):
                dve.wait_ge(sig["m_s"], t + 1)
                for g in range(BPT):
                    r = slice(g * S, (g + 1) * S)
                    dve.tensor_copy(sc[u][r, :], bT[u][r, r]).then_inc(sig["m_sc"], 1)
                dve.wait_ge(sig["m_sc"], BPT * t + BPT)
                dve.tensor_reduce(mx[u][:, 0:1], sc[u][:, :], AX.X, ALU.max).then_inc(sig["m_mx"], 1)
                dve.wait_ge(sig["m_mx"], 2 * t + 1)
                dve.tensor_scalar(mx[u][:, 1:2], mx[u][:, 0:1], -1.0 / (WS * WS * D), None, ALU.mult).then_inc(sig["m_mx"], 1)

            def soft_low(t, u):
                dve.wait_ge(sig["m_ex"], t + 1)
                dve.reciprocal(rs[u][:, 1:2], rs[u][:, 0:1]).then_inc(sig["m_an"], 1)
                dve.wait_ge(sig["m_an"], 2 * t + 1)
                dve.tensor_scalar(ex[u][:, :], ex[u][:, :], rs[u][:, 1:2], None, ALU.mult).then_inc(sig["m_an"], 1)
                dve.wait_ge(sig["m_a_hi"], BPT * t + BPT)
                for g in range(BPT):
                    r = slice(g * S, (g + 1) * S)
                    dve.tensor_tensor(aB[u][r, 1, r], ex[u][r, :], aB[u][r, 0, r], ALU.subtract).then_inc(sig["m_a_lo"], 1)

            def residual_a(t, u):
                dve.wait_ge(sig["m_ao"], t + 1)
                dve.tensor_tensor(tile(t), bA[u][:, :], tile(t), ALU.add).then_inc(sig["m_xa"], 1)
                dve.wait_ge(sig["m_xa"], t + 1)
                sig.passed(dve, "dve")
                nb.stats(dve, u, t, tile(t))

            def gate1(t, u):
                dve.wait_ge(sig["m_lg"], t + 1)
                dve.tensor_scalar(lg[u][:, 0, :], bB[u][:, 0:8], 1.0 / WS, None, ALU.mult).then_inc(sig["m_lgc"], 1)
                dve.wait_ge(sig["m_lgc"], t + 1)
                gates(sig, dve, f"m_g{u}", pair_index[0], lg[u][:, :, :], tri[:, :, :], work[u])

            def gate2(t, u):
                gates_end(sig, dve, f"m_g{u}", pair_index[0], gate[u][:, :, :], work[u])

            def down(t, u):
                dve.wait_ge(sig["m_sel"], t + 1)
                dve.tensor_copy(gsel[u][:, :], bC[u][:, 0:8]).then_inc(sig["m_gs"], 1)
                dve.wait_ge(sig["m_gs"], t + 1)
                dve.scalar_tensor_tensor(dg[u][:, :].rearrange("p (e r) -> p e r", e=E0),
                                         bA[u][:, 0:P].rearrange("p (e r) -> p e r", e=E0), 1.0 / WS,
                                         gsel[u][:, :].unsqueeze(2).broadcast_to([P, E0, R0]), ALU.mult, ALU.mult)\
                   .then_inc(sig["m_dg"], 1)

            def down_low(t, u):
                dve.wait_ge(sig["m_d_hi"], t + 1)
                dve.tensor_tensor(dT[u][:, 1, :], bT[u][:, 0:P], dT[u][:, 0, :], ALU.subtract).then_inc(sig["m_d_lo"], 1)
                dve.tensor_tensor(tile(t), tile(t), y2[u][:, :], ALU.add).then_inc(sig["m_xf"], 1)

            def residual_f(t, u):
                dve.wait_ge(sig["m_xf"], t + 1)
                dve.wait_ge(sig["m_up"], t + 1)
                dve.scalar_tensor_tensor(tile(t), bB[u][:, :], 1.0 / WS, tile(t), ALU.mult, ALU.add).then_inc(sig["m_xg"], 1)
                dve.wait_ge(sig["m_xg"], t + 1)
                sig.passed(dve, "dve")
                nq.stats(dve, u, t, tile(t))

            def q1_low(t, u):
                dve.wait_ge(sig["m_q1_hi"], CK * t + CK)
                for k in range(CK):
                    dst = XT[:, :, k, ds(t * P, P)]
                    dve.scalar_tensor_tensor(dst[:, 1, :], bC[u][:, k * P:(k + 1) * P], bias("bq1", k), dst[:, 0, :],
                                             ALU.add, ALU.subtract).then_inc(sig["m_q1_lo"], 1)

            pair_index = [None]
            stages = [residual_o, lambda t, u: na.scale(dve, u, t, tile(t), y[u][:, :]), ta.low(dve), qk_low, value,
                      value_low, soft, soft_low, residual_a, lambda t, u: nb.scale(dve, u, t, tile(t), y2[u][:, :]),
                      tb.low(dve), gate1, gate2, down, down_low, residual_f,
                      lambda t, u: nq.scale(dve, u, t, tile(t), y[u][:, :]), tq.low(dve), q1_low]
            with dve.Fori(0, NT // 2) as i:
                pair_index[0] = i
                for stage in stages:
                    for u in range(2):
                        stage(i * 2 + u, u)

        @block.scalar
        def _(act):
            load[1](act)
            act.wait_ge(sig["m_const"], 6)

            def qk_high(t, u):
                act.wait_ge(sig["m_qk"], t + 1)
                for n, (dst, b, nm) in enumerate(((qT, bB, "m_q"), (kT, bC, "m_k"))):
                    for k in range(CK):
                        act.activation(dst[u][:, 0, k, :], b[u][:, k * P:(k + 1) * P], ACT.Identity,
                                       bias=bias("bqk0", n * CK + k)).then_inc(sig[nm + "_hi"], 1)

            def value_high(t, u):
                act.wait_ge(sig["m_vz"], t + 1)
                act.activation(v[u][:, 0, :], zt[u][:, :], ACT.Copy).then_inc(sig["m_v_hi"], 1)

            def soft_exp(t, u):
                act.wait_ge(sig["m_mx"], 2 * t + 2)
                act.activation(ex[u][:, :], sc[u][:, :], ACT.Exp, bias=mx[u][:, 1:2], scale=1.0 / (WS * WS * D),
                               accum_out=rs[u][:, 0:1]).then_inc(sig["m_ex"], 1)

            def soft_high(t, u):
                act.wait_ge(sig["m_an"], 2 * t + 2)
                for g in range(BPT):
                    r = slice(g * S, (g + 1) * S)
                    act.activation(aB[u][r, 0, r], ex[u][r, :], ACT.Copy).then_inc(sig["m_a_hi"], 1)

            def gate_exp(i, u):
                act.wait_ge(sig[f"m_g{u}_sh"], i + 1)
                act.activation(work[u]["ex"], work[u]["sh"], ACT.Exp).then_inc(sig[f"m_g{u}_ex"], 1)

            def down_high(t, u):
                act.wait_ge(sig["m_dT"], t + 1)
                act.activation(dT[u][:, 0, :], bT[u][:, 0:P], ACT.Copy).then_inc(sig["m_d_hi"], 1)

            def q1_high(t, u):
                act.wait_ge(sig["m_q1"], t + 1)
                for k in range(CK):
                    act.activation(XT[:, 0, k, ds(t * P, P)], bC[u][:, k * P:(k + 1) * P], ACT.Identity,
                                   bias=bias("bq1", k)).then_inc(sig["m_q1_hi"], 1)

            with act.Fori(0, NT // 2) as i:
                for stage in (ta.high(act), qk_high, value_high, soft_exp, soft_high, tb.high(act),
                              lambda t, u: gate_exp(i, u), down_high, tq.high(act), q1_high):
                    for u in range(2):
                        stage(i * 2 + u, u)

        @block.tensor
        def _(pe):
            pe.wait_ge(*load[3])
            pe.wait_ge(sig["m_const"], 6)

            def rows_times(dst, left, w, at, n=D):
                for k in range(CK):
                    i = product(pe, dst, left(k), (w[:, 0, k, at:at + n], w[:, 1, k, at:at + n]), k == 0, k == CK - 1)
                return i

            def out_proj(t, u):
                rows_times(bA[u][:, :], lambda k: hl(XT, k, ds(t * P, P)), Wo, 0).then_inc(sig["m_o"], 1)

            def qkv(t, u):
                pe.wait_ge(sig["m_ta_lo"], t + 1)
                for dst, at in ((bB, 0), (bC, D)):
                    for m in range(CK):
                        for k in range(CK):
                            a = at + m * P
                            i = product(pe, dst[u][:, m * P:(m + 1) * P], (Wqkv[:, 0, k, a:a + P], Wqkv[:, 1, k, a:a + P]),
                                        hl(LT[u], k), k == 0, k == CK - 1)
                i.then_inc(sig["m_qk"], 1)
                rows_times(bA[u][:, :], lambda k: hl(LT[u], k), Wqkv, 2 * D).then_inc(sig["m_v"], 1)

            def scores(t, u):
                pe.wait_ge(sig["m_q_lo"], CK * t + CK)
                pe.wait_ge(sig["m_k_lo"], CK * t + CK)
                for k in range(CK):
                    i = product(pe, bT[u][:, 0:P], hl(kT[u], k), hl(qT[u], k), k == 0, k == CK - 1)
                i.then_inc(sig["m_s"], 1)

            def attend(t, u):
                pe.wait_ge(sig["m_a_lo"], BPT * t + BPT)
                pe.wait_ge(sig["m_v_lo"], t + 1)
                product(pe, bA[u][:, :], hl(aB[u]), hl(v[u])).then_inc(sig["m_ao"], 1)

            def lora_down(t, u):
                pe.wait_ge(sig["m_tb_lo"], t + 1)
                rows_times(bB[u][:, 0:8], lambda k: hl(LT[u], k), Wr, 0, 8).then_inc(sig["m_lg"], 1)
                rows_times(bA[u][:, 0:P], lambda k: hl(LT[u], k), Wd, 0, P).then_inc(sig["m_dn"], 1)

            def select(t, u):
                pe.wait_ge(sig[f"m_g{u}_gate"], pe_pair[0] + 1)
                pe.matmul(bC[u][:, 0:8], sel[:, :], gate[u][:, 0, :], start=True, stop=True).then_inc(sig["m_sel"], 1)

            def turn_down(t, u):
                pe.wait_ge(sig["m_dg"], t + 1)
                pe.transpose(bT[u][:, 0:P], dg[u][:, :], ident[:, :]).then_inc(sig["m_dT"], 1)

            def lora_up(t, u):
                pe.wait_ge(sig["m_d_lo"], t + 1)
                product(pe, bB[u][:, :], hl(dT[u]), hl(Wu, 0)).then_inc(sig["m_up"], 1)

            def queries(t, u):
                pe.wait_ge(sig["m_tq_lo"], t + 1)
                for m in range(CK):
                    for k in range(CK):
                        a = m * P
                        i = product(pe, bC[u][:, m * P:(m + 1) * P], (Wq1[:, 0, k, a:a + P], Wq1[:, 1, k, a:a + P]),
                                    hl(LT[u], k), k == 0, k == CK - 1)
                i.then_inc(sig["m_q1"], 1)

            pe_pair = [None]
            with pe.Fori(0, NT // 2) as i:
                pe_pair[0] = i
                for stage in (out_proj, ta.turn(pe), qkv, scores, attend, tb.turn(pe), lora_down, select, turn_down,
                              lora_up, tq.turn(pe), queries):
                    for u in range(2):
                        stage(i * 2 + u, u)


def walk(eng, body, before=None, after=None):
    if before:
        before()
    body(0, 0, False, True)
    with eng.Fori(0, (B - 2) // 2) as i:
        body(i * 2 + 1, 1, True, True)
        body(i * 2 + 2, 0, True, True)
    body(B - 1, 1, True, False)
    if after:
        after()


def cross1(st):
    nc, d, sig, sb = st["nc"], st["d"], st["sig"], st["sb"]
    XT, K1R, vecs, vecs16, ident = st["XT"], st["K1R"], st["vecs"], st["vecs16"], st["ident"]
    SCALE = HD1 ** -0.5 / (WS * WS)
    G = CK
    with ExitStack() as c:
        W = sb(c, "W4", [P, 2, 2 * XK * D], F16)
        Wk = W[:, :, 0:XK * D].rearrange("p a (k n) -> p a k n", k=XK)
        Wv = W[:, :, XK * D:].rearrange("p a (k n) -> p a k n", k=XK)
        xT = [sb(c, f"dx{u}", [P, XK, FULL]) for u in range(2)]
        v3 = [sb(c, f"dv3_{u}", [1, 2, D], F16) for u in range(2)]
        LT = [sb(c, f"dLT{u}", [P, 2, XK, FULL], F16) for u in range(2)]
        khat = [sb(c, f"dk{u}", [P, 2, CK, SC], F16) for u in range(2)]
        vb = [sb(c, f"dvb{u}", [P, 2, 2, D], F16) for u in range(2)]
        qbd = [sb(c, f"dq{u}", [P, 2, CK, P], F16) for u in range(2)]
        pr = sb(c, "dpr", [P, G, SC])
        mx, nm, rsum, rinv = (sb(c, n, [P, G]) for n in ("dmx", "dnm", "drsum", "drinv"))
        PT = sb(c, "dPT", [P, 2, G, 2 * P], F16)
        PTt = sb(c, "dPTt", [1, 2, G, P], F16)
        zo = sb(c, "dzo", [P, CK, S])
        ps = lambda n, s: c.enter_context(nc.psum_tensor(n, s, F32))
        pK = [ps(f"dpK{j}", [P, D]) for j in range(2)]
        pV, pO, pS = ps("dpV", [P, D]), ps("dpO", [P, G, P]), ps("dpS", [P, G, 512])
        block = c.enter_context(nc.Block())
        lc = c.enter_context(ExitStack())
        load = load_weights(st, lc, block, "w4", WAT["k1"], 2 * XK * D, W)
        hl = lambda t, *ix: (t[(slice(None), 0, *ix)], t[(slice(None), 1, *ix)])

        @block.sync
        def _(sp):
            def fetch(b, u, wait):
                if wait:
                    sp.wait_ge(sig["d_xlo"], b - 1)
                sp.dma_start(xT[u][:, :, :], d["ctxT"][ds(b, 1), :, :, :].rearrange("a p k n -> p (a k) n"))\
                  .then_inc(sig[f"d_x{u}"], 16)
                if wait:
                    sp.wait_ge(sig["d_o"], b - 1)
                sp.dma_start(v3[u][:, :, :], st["vrem1"][ds(b, 1), :].rearrange("p (a n) -> p a n", a=2))\
                  .then_inc(sig[f"d_v3_{u}"], 16)

            fetch(0, 0, False)
            fetch(1, 1, False)
            load[0](sp)
            with sp.Fori(0, (B - 2) // 2) as i:
                fetch(i * 2 + 2, 0, True)
                fetch(i * 2 + 3, 1, True)

        @block.gpsimd
        def _(pool):
            for u in range(2):
                pool.memset(qbd[u][:, :, :, :], 0.0).then_inc(sig["d_const"], 1)

            def low(b, u):
                pool.wait_ge(sig["d_xhi"], b + 1)
                pool.tensor_tensor(LT[u][:, 1, :, :], xT[u][:, :, :], LT[u][:, 0, :, :], ALU.subtract).then_inc(sig["d_xlo"], 1)

            def body(b, u, prev, nxt):
                if nxt:
                    low(b + 1, 1 - u)

            walk(pool, body, lambda: low(0, 0))

        @block.vector
        def _(dve):
            sig.begin(dve, "d_klo", "d_vlo", "d_z")
            load[2](dve)
            dve.wait_ge(sig["d_const"], 2)

            def high(b, u):
                dve.wait_ge(sig[f"d_x{u}"], 8 * b + (16 - 8 * u))
                if not isinstance(b, int) or b >= 2:
                    dve.wait_ge(sig["d_v"], 2 * b - 2)
                dve.tensor_copy(LT[u][:, 0, :, :], xT[u][:, :, :]).then_inc(sig["d_xhi"], 1)

            def key_low(b, u):
                for m in range(CK):
                    if m % 2 == 0:
                        dve.wait_ge(sig["d_khi"], CK * b + m + 2)
                    dve.scalar_tensor_tensor(khat[u][:, 1, m, 0:FULL], pK[m // 2][:, (m % 2) * FULL:(m % 2 + 1) * FULL],
                                             vecs16[:, VAT["bk1"] + m:VAT["bk1"] + m + 1], khat[u][:, 0, m, 0:FULL],
                                             ALU.add, ALU.subtract).then_inc(sig["d_klo"], 1)

            def value_low(q, u, i):
                dve.wait_ge(sig["d_vhi"], q + 1)
                dve.scalar_tensor_tensor(vb[u][:, i, 1, :], pV[:, :], 1.0 / WS, vb[u][:, i, 0, :], ALU.mult, ALU.subtract)\
                   .then_inc(sig["d_vlo"], 1)

            def gather(b, u):
                dve.tensor_copy(khat[u][:, :, :, FULL:SC], K1R[:, :, :, ds(b, 1)]).then_inc(sig["d_side"], 1)
                for j in range(BPT):
                    r = slice(j * S, (j + 1) * S)
                    dve.tensor_copy(qbd[u][r, :, :, r], XT[r, :, :, ds(b * S, S)]).then_inc(sig["d_side"], 1)

            def softmax_max(b):
                dve.wait_ge(sig["d_s"], b + 1)
                dve.tensor_reduce(mx[:, :], pS[:, :, 0:SC], AX.X, ALU.max).then_inc(sig["d_mx"], 1)
                dve.wait_ge(sig["d_mx"], b + 1)
                dve.tensor_scalar(nm[:, :], mx[:, :], -SCALE, None, ALU.mult).then_inc(sig["d_nm"], 1)

            def softmax_scale(b):
                dve.wait_ge(sig["d_exp"], G * b + G + STARTS["d_exp"])
                dve.reciprocal(rinv[:, :], rsum[:, :]).then_inc(sig["d_rinv"], 1)
                dve.wait_ge(sig["d_rinv"], b + 1)
                for g in range(G):
                    dve.tensor_scalar(pr[:, g, :], pr[:, g, :], rinv[:, g:g + 1], None, ALU.mult).then_inc(sig["d_pr"], 1)

            def probs_low(b):
                dve.wait_ge(sig["d_pthi"], 2 * b + 2)
                dve.tensor_tensor(PT[:, 1, :, :], pS[:, :, 0:2 * P], PT[:, 0, :, :], ALU.subtract).then_inc(sig["d_ptlo"], 1)
                dve.tensor_tensor(PTt[:, 1, :, :], pS[0:1, :, 2 * P:3 * P], PTt[:, 0, :, :], ALU.subtract).then_inc(sig["d_ptlo"], 1)

            def out_sum(b):
                dve.wait_ge(sig["d_o"], b + 1)
                for j in range(BPT):
                    r = slice(j * S, (j + 1) * S)
                    dve.tensor_tensor(zo[r, :, :], pO[r, :, r],
                                      vecs[r, VAT["bv1"]:VAT["bv1"] + CK].unsqueeze(2).broadcast_to([S, CK, S]), ALU.add)\
                       .then_inc(sig["d_z"], 1)

            def out_low(b):
                dve.wait_ge(sig["d_ohi"], b + 1)
                dst = XT[:, :, :, ds(b * S, S)]
                dve.tensor_tensor(dst[:, 1, :, :], zo[:, :, :], dst[:, 0, :, :], ALU.subtract).then_inc(sig["d_olo"], 1)

            def body(b, u, prev, nxt):
                if prev:
                    softmax_max(b - 1)
                if nxt:
                    high(b + 1, 1 - u)
                key_low(b, u)
                gather(b, u)
                if prev:
                    softmax_scale(b - 1)
                value_low(2 * b, u, 0)
                if prev:
                    probs_low(b - 1)
                value_low(2 * b + 1, u, 1)
                if prev:
                    out_sum(b - 1)
                    out_low(b - 1)

            def after():
                for f in (softmax_max, softmax_scale, probs_low, out_sum, out_low):
                    f(B - 1)

            walk(dve, body, lambda: high(0, 0), after)

        @block.scalar
        def _(act):
            sig.begin(act, "d_exp")
            load[1](act)

            def key_high(b, u):
                for m in range(CK):
                    if m % 2 == 0:
                        act.wait_ge(sig["d_k"], 2 * b + m // 2 + 1)
                    act.activation(khat[u][:, 0, m, 0:FULL], pK[m // 2][:, (m % 2) * FULL:(m % 2 + 1) * FULL], ACT.Identity,
                                   bias=vecs16[:, VAT["bk1"] + m:VAT["bk1"] + m + 1]).then_inc(sig["d_khi"], 1)

            def value_high(q, u, i):
                act.wait_ge(sig["d_v"], q + 1)
                act.activation(vb[u][:, i, 0, :], pV[:, :], ACT.Copy, scale=1.0 / WS).then_inc(sig["d_vhi"], 1)

            def exps(b):
                act.wait_ge(sig["d_nm"], b + 1)
                act.wait_ge(sig["d_pt"], b + STARTS["d_pt"])
                for g in range(G):
                    act.activation(pr[:, g, :], pS[:, g, 0:SC], ACT.Exp, bias=nm[:, g:g + 1], scale=SCALE,
                                   accum_out=rsum[:, g:g + 1]).then_inc(sig["d_exp"], 1)

            def probs_high(b):
                act.wait_ge(sig["d_pt"], b + 1 + STARTS["d_pt"])
                act.activation(PT[:, 0, :, :], pS[:, :, 0:2 * P], ACT.Copy).then_inc(sig["d_pthi"], 1)
                act.activation(PTt[:, 0, :, :], pS[0:1, :, 2 * P:3 * P], ACT.Copy).then_inc(sig["d_pthi"], 1)

            def out_high(b):
                act.wait_ge(sig["d_z"], BPT * b + BPT + STARTS["d_z"])
                act.activation(XT[:, 0, :, ds(b * S, S)], zo[:, :, :], ACT.Copy).then_inc(sig["d_ohi"], 1)

            def body(b, u, prev, nxt):
                if prev:
                    exps(b - 1)
                key_high(b, u)
                value_high(2 * b, u, 0)
                if prev:
                    probs_high(b - 1)
                value_high(2 * b + 1, u, 1)
                if prev:
                    out_high(b - 1)

            def after():
                for f in (exps, probs_high, out_high):
                    f(B - 1)

            walk(act, body, None, after)

        @block.tensor
        def _(pe):
            sig.begin(pe, "d_pt")
            pe.wait_ge(*load[3])

            def keys(b, u):
                pe.wait_ge(sig["d_xlo"], b + 1)
                for m in range(CK):
                    if m % 2 == 0:
                        pe.wait_ge(sig["d_klo"], (CK * b - CK + m + 2 if not isinstance(b, int) or b else 0) + STARTS["d_klo"])
                    for k in range(XK):
                        i = product(pe, pK[m // 2][:, (m % 2) * FULL:(m % 2 + 1) * FULL], hl(Wk, k, slice(m * P, (m + 1) * P)),
                                    hl(LT[u], k), k == 0, k == XK - 1)
                    if m % 2:
                        i.then_inc(sig["d_k"], 1)

            def values(q, u, i):
                pe.wait_ge(sig["d_vlo"], q + STARTS["d_vlo"])
                for k in range(XK):
                    m = product(pe, pV[:, :], hl(LT[u], k, slice(i * P, (i + 1) * P)), hl(Wv, k), k == 0, k == XK - 1)
                m.then_inc(sig["d_v"], 1)

            def scores(b, u):
                pe.wait_ge(sig["d_klo"], CK * b + CK + STARTS["d_klo"])
                pe.wait_ge(sig["d_side"], (BPT + 1) * (b + 1))
                if not isinstance(b, int) or b:
                    pe.wait_ge(sig["d_ptlo"], 2 * b)
                for g in range(G):
                    i = product(pe, pS[:, g, 0:SC], hl(qbd[u], g), hl(khat[u], g))
                i.then_inc(sig["d_s"], 1)

            def turn_probs(b):
                pe.wait_ge(sig["d_pr"], G * b + G)
                for g in range(G):
                    for i in range(2):
                        pe.transpose(pS[:, g, i * P:(i + 1) * P], pr[:, g, i * P:(i + 1) * P], ident[:, :])
                    t = pe.transpose(pS[0:1, g, 2 * P:3 * P], pr[:, g, FULL:SC], ident[:, :])
                t.then_inc(sig["d_pt"], 1)

            def outputs(b, u):
                pe.wait_ge(sig["d_ptlo"], 2 * b + 2)
                pe.wait_ge(sig["d_vlo"], 2 * b + 2 + STARTS["d_vlo"])
                pe.wait_ge(sig["d_z"], BPT * b + STARTS["d_z"])
                pe.wait_ge(sig[f"d_v3_{u}"], 8 * b + (16 - 8 * u))
                for g in range(G):
                    fs = slice(g * P, (g + 1) * P)
                    for i in range(2):
                        cs = slice(i * P, (i + 1) * P)
                        product(pe, pO[:, g, :], (vb[u][:, i, 0, fs], vb[u][:, i, 1, fs]), hl(PT, g, cs), i == 0, False)
                    m = product(pe, pO[:, g, :], (v3[u][:, 0, fs], v3[u][:, 1, fs]), hl(PTt, g), False, True)
                m.then_inc(sig["d_o"], 1)

            def body(b, u, prev, nxt):
                if prev:
                    scores(b - 1, 1 - u)
                keys(b, u)
                values(2 * b, u, 0)
                if prev:
                    turn_probs(b - 1)
                values(2 * b + 1, u, 1)
                if prev:
                    outputs(b - 1, 1 - u)

            def after():
                scores(B - 1, (B - 1) % 2)
                turn_probs(B - 1)
                outputs(B - 1, (B - 1) % 2)

            walk(pe, body, None, after)


def poly(st):
    nc, d, sig, sb = st["nc"], st["d"], st["sig"], st["sb"]
    X, XT, XR, ident, mhalf, LG = st["X"], st["XT"], st["XR"], st["ident"], st["mhalf"], st["LG"]
    MATS = 4
    with ExitStack() as c:
        cols = WAT["r1"] + CK * E1 - WAT["o1"]
        W = sb(c, "W5", [P, 2, cols], F16)
        w5 = lambda n, m: W[:, :, WAT[n] - WAT["o1"]:WAT[n] - WAT["o1"] + CK * m].rearrange("p a (k n) -> p a k n", k=CK)
        Wo, Wv, Wout, Wr = w5("o1", D), w5("pv", D), w5("out1", D), w5("r1", E1)
        Wm = [w5(n, D) for n in ("pq1", "pk1", "pq2", "pk2")]
        two = lambda n, s, dt=F32: [sb(c, f"pl_{n}{u}", s, dt) for u in range(2)]
        rows, rot, mask = sb(c, "pl_rows", [P, D]), sb(c, "pl_rot", [P, 4 * HD1 // 2]), sb(c, "pl_mask", [P, P])
        y, LT = two("y", [P, D]), two("LT", [P, 2, CK, P], F16)
        ra, rb, rr = two("ra", [P, D]), two("rb", [P, D]), two("rr", [P, D])
        mT = [two(f"mT{m}", [P, 2, CK, P], F16) for m in range(MATS)]
        v = two("v", [P, 2, D], F16)
        t1, pf = two("t1", [P, BPT, P]), two("pf", [P, BPT, P])
        pat = two("pat", [P, 2, H1, P], F16)
        yT = two("yT", [P, 2, CK, P], F16)
        banks = [c.enter_context(nc.psum_tensor(f"pl_ps{u}", [P, 4, D], F32)) for u in range(2)]
        bT, bA, bB, bC = ([b[:, n, :] for b in banks] for n in range(4))
        block = c.enter_context(nc.Block())
        lc = c.enter_context(ExitStack())
        load = load_weights(st, lc, block, "w5", WAT["o1"], cols, W)
        na, ne = Norm(sig, "p_a", st["work"]), Norm(sig, "p_e", st["work"])
        ta = Turn(sig, "p_ta", na.done, y, bT, LT, ident)
        te = Turn(sig, "p_te", ne.done, y, bT, lambda t, u: XT[:, :, :, ds(t * P, P)], ident)
        hl = lambda t, *ix: (t[(slice(None), 0, *ix)], t[(slice(None), 1, *ix)])
        tile = lambda t: X[:, ds(t, 1), :].rearrange("p a n -> p (a n)")
        heads = lambda a: a.rearrange("p (h d) -> p h d", d=HD1)
        H = HD1 // 2

        @block.sync
        def _(sp):
            sp.dma_start(rows[:, :], d["rows"][2:3, :].broadcast_to([P, D])).then_inc(sig["p_in"], 16)
            sp.dma_start(rot[:, :], d["rot"]).then_inc(sig["p_in"], 16)
            load[0](sp)

        @block.gpsimd
        def _(pool):
            pool.memset(mask[:, :], 1.0 / (HD1 * HD1)).then_inc(sig["p_const"], 1)
            pool.wait_ge(sig["p_const"], 1)
            pool.affine_select(out=mask[:, :], in_=mask[:, :], compare_op=ALU.is_ge, fill=0.0, base=0,
                               pattern=[[1, P]], channel_multiplier=-1).then_inc(sig["p_const"], 1)
            pool.wait_ge(sig["p_const"], 2)
            m4 = mask[:, :].rearrange("p (b s) -> p b s", b=BPT)
            pool.affine_select(out=m4, in_=m4, compare_op=ALU.is_ge, fill=0.0, base=0,
                               pattern=[[-S, BPT], [0, S]], channel_multiplier=1).then_inc(sig["p_const"], 1)

            def rotate(m):
                def f(t, u):
                    pool.wait_ge(sig[f"p_rb{m}"], 2 * t + 2)
                    if m:
                        pool.wait_ge(sig[f"p_mT{m - 1}"], t + 1)
                    pool.tensor_tensor(rr[u][:, :], ra[u][:, :], rb[u][:, :], ALU.add).then_inc(sig[f"p_rr{m}"], 1)
                return f

            def pattern_low(g):
                def f(t, u):
                    pool.wait_ge(sig[f"p_pathi{g}"], t + 1)
                    ps = pat[u][:, :, g * BPT:(g + 1) * BPT, :]
                    pool.tensor_tensor(ps[:, 1, :, :], pf[u][:, :, :], ps[:, 0, :, :], ALU.subtract).then_inc(sig[f"p_patlo{g}"], 1)
                return f

            def rows_low(t, u):
                pool.wait_ge(sig["p_xrhi"], t + 1)
                sig.passed(pool, "pool")
                dst = XR[:, ds(t, 1), :, :].rearrange("p a h n -> p (a h) n")
                pool.tensor_tensor(dst[:, 1, :], y[u][:, :], dst[:, 0, :], ALU.subtract).then_inc(sig["p_xrlo"], 1)

            by_pairs(pool, [lambda t, u: na.power(pool, u, t, mhalf)] + [rotate(m) for m in range(MATS)]
                     + [pattern_low(g) for g in range(CK)] + [lambda t, u: ne.power(pool, u, t, mhalf), rows_low])

        @block.vector
        def _(dve):
            load[2](dve)
            dve.wait_ge(sig["p_const"], 3)
            dve.wait_ge(sig["p_in"], 32)

            def residual_o(t, u):
                dve.tensor_tensor(tile(t), tile(t), rows[:, :], ALU.add).then_inc(sig["p_xo"], 1)
                dve.wait_ge(sig["p_xo"], 2 * t + 1)
                dve.wait_ge(sig["p_o"], t + 1)
                dve.scalar_tensor_tensor(tile(t), bA[u], 1.0 / WS, tile(t), ALU.mult, ALU.add).then_inc(sig["p_xo"], 1)
                dve.wait_ge(sig["p_xo"], 2 * t + 2)
                sig.passed(dve, "dve")
                na.stats(dve, u, t, tile(t))

            def rope(m):
                src = (bB, bC)[m % 2]

                def f(t, u):
                    dve.wait_ge(sig[f"p_m{m}"], t + 1)
                    if m:
                        dve.wait_ge(sig[f"p_rr{m - 1}"], t + 1)
                    x = heads(src[u])
                    tab = lambda a, n: rot[:, a:a + n].unsqueeze(1).broadcast_to([P, H1, n])
                    dve.tensor_tensor(heads(ra[u][:, :]), x, tab(0, HD1), ALU.mult).then_inc(sig[f"p_ra{m}"], 1)
                    dve.tensor_tensor(heads(rb[u][:, :])[:, :, 0:H], x[:, :, H:HD1], tab(HD1, H), ALU.mult).then_inc(sig[f"p_rb{m}"], 1)
                    dve.wait_ge(sig[f"p_ra{m}"], t + 1)
                    dve.tensor_tensor(heads(rb[u][:, :])[:, :, H:HD1], x[:, :, 0:H], tab(HD1 + H, H), ALU.mult).then_inc(sig[f"p_rb{m}"], 1)
                return f

            def mat_low(m):
                def f(t, u):
                    dve.wait_ge(sig[f"p_mhi{m}"], t + 1)
                    dve.tensor_tensor(mT[m][u][:, 1, :, :], bT[u].rearrange("p (k n) -> p k n", k=CK), mT[m][u][:, 0, :, :],
                                      ALU.subtract).then_inc(sig[f"p_mlo{m}"], 1)
                return f

            def value_low(t, u):
                dve.wait_ge(sig["p_vhi"], t + 1)
                dve.scalar_tensor_tensor(v[u][:, 1, :], bA[u], 1.0 / WS, v[u][:, 0, :], ALU.mult, ALU.subtract).then_inc(sig["p_vlo"], 1)

            def pattern(g):
                def f(t, u):
                    dve.wait_ge(sig[f"p_s{g // 2}"], t + 1)
                    at = (g % 2) * 2 * P
                    if g:
                        dve.wait_ge(sig[f"p_patlo{g - 1}"], t + 1)
                    dve.tensor_tensor(t1[u][:, :, :], banks[u][:, :, at:at + P],
                                      mask[:, :].unsqueeze(1).broadcast_to([P, BPT, P]), ALU.mult).then_inc(sig[f"p_t{g}"], 1)
                    dve.wait_ge(sig[f"p_t{g}"], t + 1)
                    dve.tensor_tensor(pf[u][:, :, :], banks[u][:, :, at + P:at + 2 * P], t1[u][:, :, :], ALU.mult)\
                       .then_inc(sig[f"p_pf{g}"], 1)
                return f

            def out_low(t, u):
                dve.wait_ge(sig["p_yhi"], t + 1)
                dve.tensor_tensor(yT[u][:, 1, :, :], bA[u].rearrange("p (k n) -> p k n", k=CK), yT[u][:, 0, :, :],
                                  ALU.subtract).then_inc(sig["p_ylo"], 1)

            def residual_p(t, u):
                dve.wait_ge(sig["p_out"], t + 1)
                dve.scalar_tensor_tensor(tile(t), bB[u], 1.0 / WS, tile(t), ALU.mult, ALU.add).then_inc(sig["p_xp"], 1)
                dve.wait_ge(sig["p_xp"], t + 1)
                sig.passed(dve, "dve")
                ne.stats(dve, u, t, tile(t))

            def logits(t, u):
                dve.wait_ge(sig["p_xrlo"], t + 1)
                dve.wait_ge(sig["p_lg"], t + 1)
                dve.tensor_scalar(LG[:, ds(t, 1), :].rearrange("p a e -> p (a e)"), bC[u][:, 0:E1], 1.0 / WS, None, ALU.mult)\
                   .then_inc(sig["p_lgc"], 1)

            by_pairs(dve, [residual_o, lambda t, u: na.scale(dve, u, t, tile(t), y[u][:, :]), ta.low(dve), rope(0), value_low,
                           rope(1), mat_low(0), rope(2), mat_low(1), rope(3), mat_low(2), mat_low(3)]
                     + [pattern(g) for g in range(CK)] + [out_low, residual_p,
                        lambda t, u: ne.scale(dve, u, t, tile(t), y[u][:, :]), te.low(dve), logits])

        @block.scalar
        def _(act):
            load[1](act)
            act.wait_ge(sig["p_const"], 3)

            def value_high(t, u):
                act.wait_ge(sig["p_v"], t + 1)
                act.activation(v[u][:, 0, :], bA[u], ACT.Copy, scale=1.0 / WS).then_inc(sig["p_vhi"], 1)

            def mat_high(m):
                def f(t, u):
                    act.wait_ge(sig[f"p_mT{m}"], t + 1)
                    act.activation(mT[m][u][:, 0, :, :], bT[u].rearrange("p (k n) -> p k n", k=CK), ACT.Copy).then_inc(sig[f"p_mhi{m}"], 1)
                return f

            def pattern_high(g):
                def f(t, u):
                    act.wait_ge(sig[f"p_pf{g}"], t + 1)
                    act.activation(pat[u][:, 0, g * BPT:(g + 1) * BPT, :], pf[u][:, :, :], ACT.Copy).then_inc(sig[f"p_pathi{g}"], 1)
                return f

            def out_high(t, u):
                act.wait_ge(sig["p_y"], t + 1)
                act.activation(yT[u][:, 0, :, :], bA[u].rearrange("p (k n) -> p k n", k=CK), ACT.Copy).then_inc(sig["p_yhi"], 1)

            def rows_high(t, u):
                act.wait_ge(ne.done, t + 1)
                act.activation(XR[:, ds(t, 1), 0, :].rearrange("p a n -> p (a n)"), y[u][:, :], ACT.Copy).then_inc(sig["p_xrhi"], 1)

            by_pairs(act, [ta.high(act), value_high] + [mat_high(m) for m in range(MATS)]
                     + [pattern_high(g) for g in range(CK)] + [out_high, rows_high, te.high(act)])

        @block.tensor
        def _(pe):
            pe.wait_ge(*load[3])

            def rows_times(dst, left, w, n=D):
                for k in range(CK):
                    i = product(pe, dst, left(k), hl(w, k, slice(0, n)), k == 0, k == CK - 1)
                return i

            def out_proj(t, u):
                rows_times(bA[u], lambda k: hl(XT, k, ds(t * P, P)), Wo).then_inc(sig["p_o"], 1)

            def project(m):
                dst = (bB, bC)[m % 2]

                def f(t, u):
                    if m == 0:
                        pe.wait_ge(sig["p_ta_lo"], t + 1)
                    if m >= 2:
                        pe.wait_ge(sig[f"p_rb{m - 2}"], 2 * t + 2)
                    rows_times(dst[u], lambda k: hl(LT[u], k), Wm[m]).then_inc(sig[f"p_m{m}"], 1)
                return f

            def values(t, u):
                rows_times(bA[u], lambda k: hl(LT[u], k), Wv).then_inc(sig["p_v"], 1)

            def turn_mat(m):
                def f(t, u):
                    pe.wait_ge(sig[f"p_rr{m}"], t + 1)
                    if m:
                        pe.wait_ge(sig[f"p_mlo{m - 1}"], t + 1)
                    for k in range(CK):
                        i = pe.transpose(bT[u][:, k * P:(k + 1) * P], rr[u][:, k * P:(k + 1) * P], ident[:, :])
                    i.then_inc(sig[f"p_mT{m}"], 1)
                return f

            def scores(r):
                def f(t, u):
                    if r == 0:
                        pe.wait_ge(sig["p_mlo3"], t + 1)
                        pe.wait_ge(sig["p_vlo"], t + 1)
                        pe.wait_ge(sig["p_rb3"], 2 * t + 2)
                    else:
                        pe.wait_ge(sig["p_pf1"], t + 1)
                    for g in (0, 1):
                        for s in range(2):
                            q, k = mT[2 * s][u], mT[2 * s + 1][u]
                            at = (2 * g + s) * P
                            for j in range(BPT):
                                h = slice(j * HD1, (j + 1) * HD1)
                                i = product(pe, banks[u][:, j, at:at + P], (k[h, 0, 2 * r + g, :], k[h, 1, 2 * r + g, :]),
                                            (q[h, 0, 2 * r + g, :], q[h, 1, 2 * r + g, :]))
                    i.then_inc(sig[f"p_s{r}"], 1)
                return f

            def attend(t, u):
                for g in range(CK):
                    pe.wait_ge(sig[f"p_patlo{g}"], t + 1)
                for g in range(CK):
                    for j in range(BPT):
                        h = g * BPT + j
                        i = product(pe, bA[u][j * HD1:(j + 1) * HD1, g * P:(g + 1) * P], hl(v[u], slice(h * HD1, (h + 1) * HD1)),
                                    hl(pat[u], h))
                i.then_inc(sig["p_y"], 1)

            def out_proj2(t, u):
                pe.wait_ge(sig["p_ylo"], t + 1)
                rows_times(bB[u], lambda k: hl(yT[u], k), Wout).then_inc(sig["p_out"], 1)

            def route(t, u):
                pe.wait_ge(sig["p_te_lo"], t + 1)
                rows_times(bC[u][:, 0:E1], lambda k: hl(XT, k, ds(t * P, P)), Wr, E1).then_inc(sig["p_lg"], 1)

            by_pairs(pe, [out_proj, ta.turn(pe), project(0), values, project(1), turn_mat(0), project(2), turn_mat(1), project(3),
                          turn_mat(2), turn_mat(3), scores(0), scores(1), attend, out_proj2, te.turn(pe), route])


def experts(st):
    nc, d, sig, sb = st["nc"], st["d"], st["sig"], st["sb"]
    X, XR, LG, ident = st["X"], st["XR"], st["LG"], st["ident"]
    PIECES = 12
    PW = EXPERT // PIECES
    RING = 4
    SLOTS = TOK // P
    GROUPS = IK // 2
    with ExitStack() as c:
        WB = [sb(c, f"WB{i}", [P, 2, EXPERT], F16) for i in range(2)]
        ring = [sb(c, f"e_ring{i}", [P, PW]) for i in range(RING)]
        tri, gate, gprev = sb(c, "e_tri", [P, 8, 8]), sb(c, "e_gate", [P, NT, E1]), sb(c, "e_gprev", [P, NT])
        slots = sb(c, "e_slots", [P, SLOTS, P])
        from0, own = sb(c, "e_from0", [P, P]), sb(c, "e_own", [P, NT])
        place, sel16 = sb(c, "e_place", [P, NT, E1]), sb(c, "e_sel16", [P, NT, E1], F16)
        before16, ones16, ident16 = (sb(c, f"e_{n}", [P, P], F16) for n in ("before", "ones", "ident"))
        count, tiles, over = sb(c, "e_count", [P, E1]), sb(c, "e_tiles", [P, 2 * E1 + 1]), sb(c, "e_over", [P, 8, 8])
        plan = sb(c, "e_plan", [P, 2 * E1 + 1], I32)
        pick, give = sb(c, "e_pick", [P, NT, P], F16), sb(c, "e_give", [P, NT, P], F16)
        xg = sb(c, "e_xg", [P, 2, CK, P], F16)
        sg, mf = ([sb(c, f"e_{n}{i}", [P, 2 * P]) for i in range(2)] for n in ("sg", "mf"))
        mT = sb(c, "e_mT", [P, 2, IK, P], F16)
        yo = sb(c, "e_yo", [P, 2, D], F16)
        work = gate_work(sb, c, "e_g", NT)
        ps = lambda n, s=(P, 512), dt=F32: c.enter_context(nc.psum_tensor(n, list(s), dt))
        pX = [ps(f"e_pX{i}") for i in range(2)]
        pR = [ps(f"e_pR{i}") for i in range(2)] + pX
        pT, pY = ps("e_pT", (P, NT * P), F16), ps("e_pY")
        pGU = [ps(f"e_pGU{i}") for i in range(2)]
        block = c.enter_context(nc.Block())
        hl = lambda t, *ix: (t[(slice(None), 0, *ix)], t[(slice(None), 1, *ix)])
        flat = lambda a: a.rearrange("p a n -> p (a n)")

        def number(eng, n, most):
            return eng.value_load(plan[0:1, n:n + 1] if isinstance(n, int) else plan[0:1, ds(n, 1)], min_val=0, max_val=most)

        def walk_experts(eng, tile, between=None):
            def expert(e, w, nxt):
                here, ahead = number(eng, e, SLOTS), number(eng, e + E1, 3 * E1)
                for s in range(2):
                    pieces = range(s * PIECES // 2, (s + 1) * PIECES // 2) if nxt else ()
                    with eng.If(here > s):
                        tile(ahead + s, s, e, w, pieces)
                    if between and nxt:
                        with eng.Else():
                            between(ahead + s, e, w, pieces)
                with eng.Fori(0, SLOTS - 2) as s:
                    with eng.If(here > s + 2):
                        tile(ahead + s + 2, s + 2, e, w, ())

            with eng.Fori(0, E1 // 2 - 1) as i:
                expert(i * 2, 0, True)
                expert(i * 2 + 1, 1, True)
            expert(E1 - 2, 0, True)
            expert(E1 - 1, 1, False)

        @block.sync
        def _(sp):
            def load(e, first):
                for n in range(PIECES):
                    if not first or n >= RING:
                        sp.wait_ge(sig["e_wlo"], e * PIECES + n - RING + 1)
                    sp.dma_start(ring[n % RING][:, :], d["WE"][ds(e, 1), :, n * PW:(n + 1) * PW].rearrange("a p n -> p (a n)"))\
                      .then_inc(sig[f"e_came{n % RING}"], 16)

            sp.dma_start(flat(slots[:, :, :]), d["slots"].broadcast_to([P, TOK])).then_inc(sig["e_slots"], 16)
            load(0, True)
            with sp.Fori(0, E1 - 1) as i:
                load(i + 1, False)
            sp.wait_ge(sig["e_end"], 1)
            sp.dma_start(st["out"].rearrange("(t p) n -> p t n", p=P), X[:, :, :]).then_inc(sig["e_out"], 16)
            sp.wait_ge(sig["e_out"], 16)

        @block.gpsimd
        def _(pool):
            pool.memset(tri[:, :, :], 1.0).then_inc(sig["e_const"], 1)
            pool.memset(before16[:, :], 1.0).then_inc(sig["e_const"], 1)
            pool.memset(ones16[:, :], 1.0).then_inc(sig["e_const"], 1)
            pool.memset(gprev[:, :], 0.0).then_inc(sig["e_const"], 1)
            pool.memset(yo[:, :, :], 0.0).then_inc(sig["e_const"], 1)
            pool.memset(give[:, :, :], 0.0).then_inc(sig["e_const"], 1)
            pool.tensor_copy(ident16[:, :], ident[:, :]).then_inc(sig["e_const"], 1)
            pool.wait_ge(sig["e_const"], 7)
            pool.affine_select(out=tri[:, :, :], in_=tri[:, :, :], compare_op=ALU.is_gt, fill=0.0, base=0,
                               pattern=[[1, 8], [-1, 8]], channel_multiplier=0).then_inc(sig["e_const"], 1)
            pool.affine_select(out=before16[:, :], in_=before16[:, :], compare_op=ALU.is_gt, fill=0.0, base=0,
                               pattern=[[1, P]], channel_multiplier=-1).then_inc(sig["e_const"], 1)
            pool.wait_ge(sig["e_slots"], 16)
            pool.tensor_scalar(from0[:, :], slots[:, 0, :], 1.0, None, ALU.subtract).then_inc(sig["e_own0"], 1)
            pool.wait_ge(sig["e_own0"], 1)
            pool.wait_ge(sig["e_plan"], 1)

            def tile(j, s, e, w, pieces):
                pool.wait_ge(sig["e_turned"], j + STARTS["e_turned"])
                sig.passed(pool, "pool")
                first = slots[:, s, 0:1] if isinstance(s, int) else slots[:, ds(s, 1), 0:1].rearrange("p a n -> p (a n)")
                chosen = place[:, :, e:e + 1] if isinstance(e, int) else place[:, :, ds(e, 1)]
                pool.tensor_tensor(own[:, :], chosen.rearrange("p t a -> p (t a)"), first.broadcast_to([P, NT]), ALU.subtract)\
                    .then_inc(sig["e_own"], 1)
                pool.wait_ge(sig["e_own"], j + 1)
                sig.passed(pool, "pool")
                for t in range(NT):
                    i = pool.tensor_scalar(pick[:, t, :], from0[:, :], own[:, t:t + 1], None, ALU.is_equal)
                i.then_inc(sig["e_pick"], 1)
                for g in range(GROUPS):
                    pool.wait_ge(sig["e_mhi"], j * GROUPS + g + 1)
                    pool.tensor_tensor(mT[:, 1, 2 * g:2 * g + 2, :], mf[g % 2][:, :].rearrange("p (a n) -> p a n", a=2),
                                       mT[:, 0, 2 * g:2 * g + 2, :], ALU.subtract).then_inc(sig["e_mlo"], 1)

            walk_experts(pool, tile)

        @block.vector
        def _(dve):
            sig.begin(dve, "e_mf", "e_x", "e_ylo")
            dve.wait_ge(sig["e_const"], 9)
            dve.wait_ge(sig["e_slots"], 16)
            gates(sig, dve, "e_g", 0, LG[:, :, :], tri[:, :, :], work)
            dve.wait_ge(sig["e_g"], 7)
            dve.tensor_copy(sel16[:, :, :], work["sel"]).then_inc(sig["e_sel16"], 1)
            gates_end(sig, dve, "e_g", 0, gate[:, :, :], work)
            dve.wait_ge(sig["e_g_gate"], 1)
            dve.tensor_scalar(gate[:, :, :], gate[:, :, :], 1.0 / WS, None, ALU.mult).then_inc(sig["e_gs"], 1)
            dve.wait_ge(sig["e_gs"], 1)
            dve.wait_ge(sig["e_counted"], 1)
            dve.scalar_tensor_tensor(flat(place[:, :, :]), pR[0][:, 0:NT * E1], 1.0, flat(work["sel"]), ALU.add, ALU.mult)\
               .then_inc(sig["e_plans"], 1)
            dve.tensor_copy(count[:, :], pR[1][:, 0:E1]).then_inc(sig["e_plans"], 1)
            dve.wait_ge(sig["e_plans"], 2)
            dve.tensor_tensor(over[:, :, :], count[:, :].unsqueeze(2).broadcast_to([P, E1, SLOTS]),
                              slots[:, :, 0].unsqueeze(1).broadcast_to([P, E1, SLOTS]), ALU.is_ge).then_inc(sig["e_plans"], 1)
            dve.wait_ge(sig["e_plans"], 3)
            dve.tensor_reduce(tiles[:, 0:E1], over[:, :, :], AX.X, ALU.add).then_inc(sig["e_plans"], 1)
            dve.wait_ge(sig["e_plans"], 4)
            dve.tensor_tensor(over[:, :, :], tri[:, :, :], tiles[:, 0:E1].unsqueeze(1).broadcast_to([P, E1, E1]), ALU.mult)\
               .then_inc(sig["e_plans"], 1)
            dve.tensor_reduce(tiles[:, 2 * E1:2 * E1 + 1], tiles[:, 0:E1], AX.X, ALU.add).then_inc(sig["e_plans"], 1)
            dve.wait_ge(sig["e_plans"], 6)
            dve.tensor_reduce(tiles[:, E1:2 * E1], over[:, :, :], AX.X, ALU.add).then_inc(sig["e_plans"], 1)
            dve.wait_ge(sig["e_plans"], 7)
            dve.tensor_copy(plan[:, :], tiles[:, :]).then_inc(sig["e_plan"], 1)
            dve.wait_ge(sig["e_plan"], 1)

            def split(e, w, n):
                dve.wait_ge(sig["e_whi"], e * PIECES + n + 1)
                a = slice(n * PW, (n + 1) * PW)
                dve.scalar_tensor_tensor(WB[w][:, 1, a], ring[n % RING][:, :], WS, WB[w][:, 0, a], ALU.mult, ALU.subtract)\
                   .then_inc(sig["e_wlo"], 1)

            def hand_back(j):
                for t in range(NT):
                    dve.wait_ge(sig["e_back"], j * NT + t + 1)
                    dve.scalar_tensor_tensor(X[:, t, :], pR[t % 4][:, :], gprev[:, t:t + 1], X[:, t, :], ALU.mult, ALU.add)\
                       .then_inc(sig["e_x"], 1)

            def tile(j, s, e, w, pieces):
                dve.wait_ge(sig["e_gathered"], j + 1)
                dve.tensor_copy(xg[:, 1, :, :], pX[1][:, :].rearrange("p (k n) -> p k n", k=CK)).then_inc(sig["e_xlo"], 1)
                hand_back(j)
                dve.wait_ge(sig["e_x"], j * NT + NT + STARTS["e_x"])
                own = gate[:, :, e:e + 1] if isinstance(e, int) else gate[:, :, ds(e, 1)]
                dve.tensor_copy(gprev[:, :].unsqueeze(2), own).then_inc(sig["e_gate"], 1)
                dve.wait_ge(sig["e_gate"], j + 1)
                for g in range(GROUPS):
                    dve.wait_ge(sig["e_sg"], j * GROUPS + g + 1)
                    dve.wait_ge(sig["e_mlo"], j * GROUPS + g)
                    dve.scalar_tensor_tensor(mf[g % 2][:, :], pGU[g % 2][:, 2 * P:4 * P], 1.0 / WS, sg[g % 2][:, :], ALU.mult, ALU.mult)\
                       .then_inc(sig["e_mf"], 1)
                    if pieces:
                        split(e + 1, 1 - w, pieces[g])
                dve.wait_ge(sig["e_yhi"], j + 1)
                dve.tensor_tensor(yo[:, 1, :], pY[:, :], yo[:, 0, :], ALU.subtract).then_inc(sig["e_ylo"], 1)
                for n in pieces[GROUPS:]:
                    split(e + 1, 1 - w, n)

            def between(j, e, w, pieces):
                for n in pieces:
                    split(e + 1, 1 - w, n)

            for n in range(PIECES):
                split(0, 0, n)
            walk_experts(dve, tile, between)
            total = number(dve, 2 * E1, 3 * E1)
            hand_back(total)
            dve.wait_ge(sig["e_x"], total * NT + NT + STARTS["e_x"])
            dve.sem_inc(sig["e_end"], 1)

        @block.scalar
        def _(act):
            sig.begin(act, "e_given")
            act.wait_ge(sig["e_g_sh"], 1)
            act.activation(work["ex"], work["sh"], ACT.Exp).then_inc(sig["e_g_ex"], 1)

            def split(e, w, n):
                act.wait_ge(sig[f"e_came{n % RING}"], e * (16 * PIECES // RING) + 16 * (n // RING + 1))
                a = slice(n * PW, (n + 1) * PW)
                act.activation(WB[w][:, 0, a], ring[n % RING][:, :], ACT.Copy, scale=WS).then_inc(sig["e_whi"], 1)

            def tile(j, s, e, w, pieces):
                act.wait_ge(sig["e_gathered"], j + 1)
                act.activation(xg[:, 0, :, :], pX[0][:, :].rearrange("p (k n) -> p k n", k=CK), ACT.Copy).then_inc(sig["e_xhi"], 1)
                act.wait_ge(sig["e_back"], j * NT + NT)
                act.activation(flat(give[:, :, :]), pT[:, :], ACT.Copy).then_inc(sig["e_given"], 1)
                for g in range(GROUPS):
                    act.wait_ge(sig["e_gu"], j * GROUPS + g + 1)
                    act.activation(sg[g % 2][:, :], pGU[g % 2][:, 0:2 * P], ACT.Silu, scale=1.0 / WS).then_inc(sig["e_sg"], 1)
                    act.wait_ge(sig["e_mf"], j * GROUPS + g + 1 + STARTS["e_mf"])
                    act.activation(mT[:, 0, 2 * g:2 * g + 2, :], mf[g % 2][:, :].rearrange("p (a n) -> p a n", a=2), ACT.Copy)\
                       .then_inc(sig["e_mhi"], 1)
                    if pieces:
                        split(e + 1, 1 - w, pieces[g])
                act.wait_ge(sig["e_down"], j + 1 + STARTS["e_down"])
                act.activation(yo[:, 0, :], pY[:, :], ACT.Copy).then_inc(sig["e_yhi"], 1)
                for n in pieces[GROUPS:]:
                    split(e + 1, 1 - w, n)

            def between(j, e, w, pieces):
                act.wait_ge(sig["e_down"], j + STARTS["e_down"] if pieces[0] == 0 else 1)
                for n in pieces:
                    split(e + 1, 1 - w, n)

            for n in range(PIECES):
                split(0, 0, n)
            act.wait_ge(sig["e_plan"], 1)
            walk_experts(act, tile, between)

        @block.tensor
        def _(pe):
            sig.begin(pe, "e_turned", "e_down")
            pe.wait_ge(sig["e_const"], 9)
            pe.wait_ge(sig["e_sel16"], 1)
            pe.matmul(pR[0][:, 0:NT * E1], before16[:, :], flat(sel16[:, :, :]), start=True, stop=False)
            for t in range(NT - 1):
                n = NT - 1 - t
                pe.matmul(pR[0][:, (t + 1) * E1:NT * E1].rearrange("p (t e) -> p t e", e=E1), ones16[:, :],
                          sel16[:, t:t + 1, :].broadcast_to([P, n, E1]), start=False, stop=t == NT - 2)
            for t in range(NT):
                i = pe.matmul(pR[1][:, 0:E1], ones16[:, :], sel16[:, t, :], start=t == 0, stop=t == NT - 1)
            i.then_inc(sig["e_counted"], 1)
            pe.wait_ge(sig["e_plan"], 1)

            def hand_back(j):
                pe.wait_ge(sig["e_ylo"], j + STARTS["e_ylo"])
                pe.wait_ge(sig["e_given"], j + STARTS["e_given"])
                for t in range(NT):
                    pe.wait_ge(sig["e_x"], j * NT + max(t - 3, 0) + STARTS["e_x"])
                    for part in range(2):
                        i = pe.matmul(pR[t % 4][:, :], give[:, t, :], yo[:, part, :], start=part == 0, stop=part == 1)
                    i.then_inc(sig["e_back"], 1)

            def tile(j, s, e, w, pieces):
                pe.wait_ge(sig["e_pick"], j + 1)
                pe.wait_ge(sig["e_x"], j * NT + STARTS["e_x"])
                for part in range(2):
                    for k in range(CK):
                        for t in range(NT):
                            i = pe.matmul(pX[part][:, k * P:(k + 1) * P], XR[:, t, part, k * P:(k + 1) * P], pick[:, t, :],
                                          start=t == 0, stop=t == NT - 1)
                i.then_inc(sig["e_gathered"], 1)
                pe.wait_ge(sig["e_given"], j + STARTS["e_given"])
                for t in range(NT):
                    i = pe.transpose(pT[:, t * P:(t + 1) * P], pick[:, t, :], ident16[:, :])
                i.then_inc(sig["e_turned"], 1)
                pe.wait_ge(sig["e_xhi"], j + 1)
                pe.wait_ge(sig["e_xlo"], j + 1)
                hand_back(j)
                wg, wu, wd = (WB[w][:, :, a * CK * INTER:(a + 1) * CK * INTER] for a in range(3))
                wg, wu = (x.rearrange("p a (k n) -> p a k n", k=CK) for x in (wg, wu))
                wd = wd.rearrange("p a (k n) -> p a k n", k=IK)
                pe.wait_ge(sig["e_wlo"], e * PIECES + PIECES)
                for g in range(GROUPS):
                    pe.wait_ge(sig["e_mf"], j * GROUPS + g - 1 + STARTS["e_mf"])
                    for n, wt in enumerate((wg, wg, wu, wu)):
                        m = 2 * g + n % 2
                        for k in range(CK):
                            i = product(pe, pGU[g % 2][:, n * P:(n + 1) * P], hl(wt, k, slice(m * P, (m + 1) * P)), hl(xg, k),
                                        k == 0, k == CK - 1)
                    i.then_inc(sig["e_gu"], 1)
                for k in range(IK):
                    if k % 2 == 0:
                        pe.wait_ge(sig["e_mlo"], j * GROUPS + k // 2 + 1)
                    i = product(pe, pY[:, :], hl(mT, k), hl(wd, k), k == 0, k == IK - 1)
                i.then_inc(sig["e_down"], 1)

            walk_experts(pe, tile)
            hand_back(number(pe, 2 * E1, 3 * E1))


def pack(w):
    n = w.shape[0] // P
    return np.ascontiguousarray(w.reshape(n, P, w.shape[1]).transpose(1, 0, 2)).reshape(P, n * w.shape[1])


def columns(v):
    return v.reshape(-1, P).T


def rotary():
    inv = (1.0 / np.float32(10000.0) ** (np.arange(0, HD1, 2, dtype=np.float32) / np.float32(HD1))).astype(np.float32)
    freq = np.arange(S, dtype=np.float32)[:, None] * inv[None, :]

    def to_bfloat16(v):
        bits = v.view(np.uint32)
        return ((bits + np.uint32(0x7FFF) + ((bits >> 16) & np.uint32(1))) & np.uint32(0xFFFF0000)).view(np.float32)

    cos, sin = to_bfloat16(np.cos(freq)), to_bfloat16(np.sin(freq))
    both = np.concatenate([cos, cos, sin, -sin], axis=1) / np.float32(WS)
    return np.tile(both, (BPT, 1)).astype(np.float32)


def kernel(**inputs):
    import concourse.bacc as bacc
    from concourse.bass_utils import run_bass_kernel_spmd

    a = {k: np.asarray(v) for k, v in inputs.items()}
    ctx_t = a["ctx_768"].transpose(0, 2, 1)
    weights = {
        "q0": a["L0_xattn_Wq"].T, "kv0": a["L0_xattn_Wkv"].T, "lkv0": a["L0_xattn_Wlkv"].T, "o0": a["L0_xattn_Wo"].T,
        "qkv0": a["L0_attn_W"].T, "down": a["L0_ffn_lora_down"].reshape(E0 * R0, D).T,
        "up": a["L0_ffn_lora_up"].transpose(0, 2, 1).reshape(E0 * R0, D), "r0": a["L0_ffn_router_w"].T,
        "q1": a["L1_xattn_Wq"], "k1": a["L1_xattn_Wk"], "v1": a["L1_xattn_Wv"], "o1": a["L1_xattn_Wo"],
        "pq1": a["L1_attn_Wq1"].T, "pk1": a["L1_attn_Wk1"].T, "pq2": a["L1_attn_Wq2"].T, "pk2": a["L1_attn_Wk2"].T,
        "pv": a["L1_attn_Wv"].T, "out1": a["L1_attn_Wout"].T, "r1": a["L1_ffn_router_w"].T,
    }
    vectors = {
        "lng": columns(a["L0_xattn_ln_l_g"]), "lnb": columns(a["L0_xattn_ln_l_b"]),
        "lxg": columns(a["L0_xattn_ln_x_g"]), "lxb": columns(a["L0_xattn_ln_x_b"]),
        "qg": np.concatenate([a["L0_xattn_qn_g"]] * 2)[:, None], "kg": np.concatenate([a["L0_xattn_kn_g"]] * 2)[:, None],
        "bqk0": columns(a["L0_attn_b"][:2 * D]), "bq1": columns(a["L1_xattn_bq"]), "bk1": columns(a["L1_xattn_bk"]),
        "bv1": columns(a["L1_xattn_bv"]),
    }
    arrays = {
        "x": a["x"].reshape(TOK, D),
        "ctx": a["ctx_768"],
        "ctxT": ctx_t[:, :, :FULL].reshape(B, XK, P, FULL).transpose(0, 2, 1, 3),
        "rem": a["ctx_768"][:, FULL, :],
        "remT": ctx_t[:, :, FULL].reshape(B, XK, P).transpose(2, 1, 0),
        "mask": a["mask_BxS2_bk0"].reshape(1, B, SC),
        "vecs": np.concatenate([vectors[n] for n, _ in VCOLS], axis=1),
        "rows": np.stack([a["L0_xattn_bo"], a["L0_attn_b"][2 * D:], a["L1_xattn_bo"]]),
        "rot": rotary(),
        "slots": np.arange(1, TOK + 1, dtype=np.float32)[None, :],
        "W": np.concatenate([pack(weights[n]) for n, _ in WCOLS], axis=1),
        "WE": np.stack([np.concatenate([pack(a["L1_ffn_wg"][e].T), pack(a["L1_ffn_wu"][e].T), pack(a["L1_ffn_wd"][e].T)],
                                       axis=1) for e in range(E1)]),
    }
    nc = bacc.Bacc("TRN2", target_bir_lowering=False, num_devices=1)
    d, given = {}, {}
    for name, value in arrays.items():
        given[f"in_{name}"] = np.ascontiguousarray(value)
        d[name] = nc.dram_tensor(f"in_{name}", value.shape, mybir.dt.from_np(value.dtype), kind="ExternalInput").ap()
    out = nc.dram_tensor("out_y", (TOK, D), F32, kind="ExternalOutput").ap()
    perceiver(nc, d, out)
    r = run_bass_kernel_spmd(nc, [given], core_ids=[0])
    return r.results[0]["out_y"].reshape(B, S, D)
```
